# Optimizing a Trainium2 kernel written in Bass

```python
import numpy as np
import jax
import jax.numpy as jnp

def _softmax(x, axis=-1):
    return jax.nn.softmax(x, axis=axis)

def _gelu(x):
    return jax.nn.gelu(x, approximate=True)

def _silu(x):
    return jax.nn.silu(x)

def _sigmoid(x):
    return jax.nn.sigmoid(x)

def _layernorm(x, axis=-1, eps=1e-05):
    m = jnp.mean(x, axis=axis, keepdims=True)
    v = jnp.var(x, axis=axis, keepdims=True)
    return (x - m) / jnp.sqrt(v + eps)

def _scatter_add(tgt, idx, src, axis=0):
    return tgt.at[idx].add(src)

def _segment_sum(src, seg, n):
    return jax.ops.segment_sum(src, seg, n)
kernel_name = 'mk_decoder_postln_d1_seqx_r8_88abc5'

def setup_inputs(seed: int=0):
    np.random.seed(seed)
    _w = jnp.asarray

    def _rec_inputs():
        import jax
        import jax.numpy as jnp
        _rk = jax.random.key(seed)
        x = 7.22e-05 + 1 * jax.random.normal(jax.random.fold_in(_rk, 1), (4, 256, 256), jnp.float32)
        _lenS = 256 - jax.random.randint(jax.random.fold_in(_rk, 7), (4,), 0, max(1, 256 // 4) + 1, jnp.int32)
        _lenS2 = 256 - jax.random.randint(jax.random.fold_in(_rk, 8), (4,), 0, max(1, 256 // 4) + 1, jnp.int32)
        _ctx_2048P = jax.random.normal(jax.random.fold_in(_rk, 11), (4, 16, 256), jnp.float32)
        _ctx_2048c = jax.random.dirichlet(jax.random.fold_in(_rk, 511), 0.3 * jnp.ones((16,), jnp.float32), (4, 256))
        _ctx_2048t = jnp.einsum('bsk,bkd->bsd', _ctx_2048c, _ctx_2048P)
        _ctx_2048t = _ctx_2048t * jax.lax.rsqrt(jnp.mean(jnp.square(_ctx_2048t)) + 1e-12) * 0.953939
        ctx_2048 = 4.13588e-05 + 0.999923 * (_ctx_2048t + 0.3 * jax.random.normal(jax.random.fold_in(_rk, 611), (4, 256, 256), jnp.float32))
        return (x, ctx_2048)
    x, ctx_2048 = _rec_inputs()

    def _L0_attn_setup():
        import jax, jax.numpy as jnp
        import numpy as np
        E2M1_GRID = jnp.array([0.0, 0.5, 1.0, 1.5, 2.0, 3.0, 4.0, 6.0], dtype=jnp.float32)
        E2M1_MIDS = (E2M1_GRID[1:] + E2M1_GRID[:-1]) / 2.0
        FP4_MAX = 6.0
        FP8_E4M3_MAX = 448.0

        def nvfp4_quant_dequant(w):
            O, I = w.shape
            w16 = w.reshape(O, I // 128, 8, 16)
            amax128 = jnp.max(jnp.abs(w16), axis=(-2, -1))
            outer = amax128 / (FP4_MAX * FP8_E4M3_MAX)
            outer = jnp.where(outer > 0, outer, 1.0)
            amax16 = jnp.max(jnp.abs(w16), axis=-1)
            inner = amax16 / FP4_MAX / outer[..., None]
            inner = inner.astype(jnp.float8_e4m3fn).astype(jnp.float32)
            scale = outer[..., None] * inner
            safe = jnp.where(scale > 0, scale, 1.0)[..., None]
            code = w16 / safe
            a = jnp.abs(code)
            idx = jnp.searchsorted(E2M1_MIDS, a)
            q = E2M1_GRID[idx] * jnp.sign(code)
            return (q * scale[..., None]).reshape(O, I)
        key = jax.random.key(seed)
        k0, k1, k2 = jax.random.split(key, 3)
        B, S, H = (2, 256, 256)
        hidden_states = jax.random.normal(k0, (B, S, H), dtype=jnp.float32)
        w_qkv = jax.random.normal(k1, (3 * H, H), dtype=jnp.float32) * 0.023
        w_o = jax.random.normal(k2, (H, H), dtype=jnp.float32) * 0.023
        w_qkv = nvfp4_quant_dequant(w_qkv)
        w_o = nvfp4_quant_dequant(w_o)
        return {'hidden_states': hidden_states, 'w_qkv': w_qkv, 'w_o': w_o}
    _L0_attn_all = _L0_attn_setup()
    _L0_attn_in = {k: v for k, v in _L0_attn_all.items() if k in ('w_qkv', 'w_o')}
    del _L0_attn_all

    def _L0_xattn_setup():
        import jax, jax.numpy as jnp
        import numpy as np
        B, S, DIM, HD = (4, 128, 256, 128)
        H = DIM // HD
        GN_EPS = 0.001

        def _decay_masks(n_heads, seq_len):
            gam = 1.0 - 2.0 ** (-5.0 - jnp.arange(n_heads, dtype=jnp.float32))
            idx = jnp.arange(seq_len, dtype=jnp.float32)
            expo = idx[None, :] - idx[:, None]
            D = jnp.where(expo[None, :, :] <= 0, gam[:, None, None] ** expo[None, :, :], 0.0)
            return D / jnp.sqrt(D.sum(axis=-1))[:, None, :]
        key = jax.random.key(seed)
        ks = jax.random.split(key, 8)
        x = jax.random.normal(ks[0], (B, S, DIM), dtype=jnp.float32)
        k = jax.random.normal(ks[1], (B, S, DIM), dtype=jnp.float32)
        v = jax.random.normal(ks[2], (B, S, DIM), dtype=jnp.float32)
        Wh = jax.random.normal(ks[3], (H, HD, HD), dtype=jnp.float32) / np.sqrt(HD)
        wg_w = jax.random.normal(ks[4], (DIM, DIM), dtype=jnp.float32) / np.sqrt(DIM)
        wo_w = jax.random.normal(ks[5], (DIM, DIM), dtype=jnp.float32) / np.sqrt(DIM)
        gn_gamma = jnp.ones((DIM,), dtype=jnp.float32)
        gn_beta = jnp.zeros((DIM,), dtype=jnp.float32)
        return {'x': x, 'k': k, 'v': v, 'Wh': Wh, 'wg_w': wg_w, 'wo_w': wo_w, 'gn_gamma': gn_gamma, 'gn_beta': gn_beta}
    _L0_xattn_all = _L0_xattn_setup()
    _L0_xattn_in = {k: v for k, v in _L0_xattn_all.items() if k in ('Wh', 'wg_w', 'wo_w', 'gn_gamma', 'gn_beta')}
    del _L0_xattn_all

    def _L0_ffn_setup():
        import jax, jax.numpy as jnp
        import numpy as np
        TOPK = 4
        key = jax.random.key(seed)
        k_x, k_a, k_b, k_w, k_bias = jax.random.split(key, 5)
        b, s, h, j, a, r = (4, 256, 256, 256, 64, 16)
        x = jax.random.normal(k_x, (b, s, h), dtype=jnp.float32)
        A = jax.random.normal(k_a, (a, r, h), dtype=jnp.float32) * 0.02
        B = jax.random.normal(k_b, (a, j, r), dtype=jnp.float32) * 0.02
        W = jax.random.normal(k_w, (j, h), dtype=jnp.float32) * 0.02
        bias = jax.random.normal(k_bias, (j,), dtype=jnp.float32) * 0.02
        return {'x': x, 'A': A, 'B': B, 'W': W, 'bias': bias}
    _L0_ffn_all = _L0_ffn_setup()
    _L0_ffn_in = {k: v for k, v in _L0_ffn_all.items() if k in ('A', 'B', 'W', 'bias')}
    del _L0_ffn_all
    return {'x': x, 'ctx_2048': ctx_2048, 'L0_attn_w_qkv': _L0_attn_in['w_qkv'], 'L0_attn_w_o': _L0_attn_in['w_o'], 'L0_xattn_Wh': _L0_xattn_in['Wh'], 'L0_xattn_wg_w': _L0_xattn_in['wg_w'], 'L0_xattn_wo_w': _L0_xattn_in['wo_w'], 'L0_xattn_gn_gamma': _L0_xattn_in['gn_gamma'], 'L0_xattn_gn_beta': _L0_xattn_in['gn_beta'], 'L0_ffn_A': _L0_ffn_in['A'], 'L0_ffn_B': _L0_ffn_in['B'], 'L0_ffn_W': _L0_ffn_in['W'], 'L0_ffn_bias': _L0_ffn_in['bias']}

def reference(x, ctx_2048, L0_attn_w_qkv, L0_attn_w_o, L0_xattn_Wh, L0_xattn_wg_w, L0_xattn_wo_w, L0_xattn_gn_gamma, L0_xattn_gn_beta, L0_ffn_A, L0_ffn_B, L0_ffn_W, L0_ffn_bias):
    import jax
    import jax.numpy as jnp

    def _L0_attn_ref(hidden_states, w_qkv, w_o):
        import jax, jax.numpy as jnp
        import numpy as np
        E2M1_GRID = jnp.array([0.0, 0.5, 1.0, 1.5, 2.0, 3.0, 4.0, 6.0], dtype=jnp.float32)
        E2M1_MIDS = (E2M1_GRID[1:] + E2M1_GRID[:-1]) / 2.0
        FP4_MAX = 6.0
        FP8_E4M3_MAX = 448.0

        def nvfp4_quant_dequant(w):
            O, I = w.shape
            w16 = w.reshape(O, I // 128, 8, 16)
            amax128 = jnp.max(jnp.abs(w16), axis=(-2, -1))
            outer = amax128 / (FP4_MAX * FP8_E4M3_MAX)
            outer = jnp.where(outer > 0, outer, 1.0)
            amax16 = jnp.max(jnp.abs(w16), axis=-1)
            inner = amax16 / FP4_MAX / outer[..., None]
            inner = inner.astype(jnp.float8_e4m3fn).astype(jnp.float32)
            scale = outer[..., None] * inner
            safe = jnp.where(scale > 0, scale, 1.0)[..., None]
            code = w16 / safe
            a = jnp.abs(code)
            idx = jnp.searchsorted(E2M1_MIDS, a)
            q = E2M1_GRID[idx] * jnp.sign(code)
            return (q * scale[..., None]).reshape(O, I)
        B, S, H = hidden_states.shape
        num_heads = 16
        head_dim = H // num_heads
        qkv = jnp.einsum('bsh,oh->bso', hidden_states, w_qkv)
        qkv = qkv.reshape(B, S, 3, num_heads, head_dim)
        qkv = jnp.transpose(qkv, (2, 0, 3, 1, 4))
        q, k, v = (qkv[0], qkv[1], qkv[2])
        scale = 1.0 / jnp.sqrt(jnp.float32(head_dim))
        scores = jnp.einsum('bhqd,bhkd->bhqk', q, k) * scale
        causal = jnp.tril(jnp.ones((S, S), dtype=bool))
        scores = jnp.where(causal, scores, jnp.finfo(scores.dtype).min)
        probs = jax.nn.softmax(scores, axis=-1)
        attn = jnp.einsum('bhqk,bhkd->bhqd', probs, v)
        attn = jnp.transpose(attn, (0, 2, 1, 3)).reshape(B, S, H)
        return jnp.einsum('bsh,oh->bso', attn, w_o)

    def _L0_xattn_ref(x, k, v, Wh, wg_w, wo_w, gn_gamma, gn_beta):
        import jax, jax.numpy as jnp
        import numpy as np
        B, S, DIM, HD = (4, 128, 256, 128)
        H = DIM // HD
        GN_EPS = 0.001

        def _decay_masks(n_heads, seq_len):
            gam = 1.0 - 2.0 ** (-5.0 - jnp.arange(n_heads, dtype=jnp.float32))
            idx = jnp.arange(seq_len, dtype=jnp.float32)
            expo = idx[None, :] - idx[:, None]
            D = jnp.where(expo[None, :, :] <= 0, gam[:, None, None] ** expo[None, :, :], 0.0)
            return D / jnp.sqrt(D.sum(axis=-1))[:, None, :]
        b, s, dim = x.shape
        h, hd, _ = Wh.shape
        xh = x.reshape(b, s, h, hd)
        kh = k.reshape(b, s, h, hd)
        vh = v.reshape(b, s, h, hd)
        Q = jnp.einsum('bshd,hde->bshe', xh, Wh)
        K = jnp.einsum('bshd,hde->bshe', kh, Wh)
        V = jnp.einsum('bshd,hde->bshe', vh, Wh)
        scores = jnp.einsum('bshe,bthe->bhst', Q, K) / jnp.sqrt(jnp.float32(hd))
        Dn = _decay_masks(h, s)
        masked = scores * Dn[None, :, :, :]
        A = jnp.maximum(jnp.abs(masked.sum(axis=0)), 1.0)
        O = jnp.einsum('hst,bthe->bshe', A, V).reshape(b, s, dim)
        mu = O.mean(axis=-1, keepdims=True)
        var = O.var(axis=-1, keepdims=True)
        Y = (O - mu) / jnp.sqrt(var + GN_EPS) * gn_gamma + gn_beta
        W = jax.nn.relu(x @ wg_w)
        return W * Y @ wo_w

    def _L0_ffn_ref(x, A, B, W, bias):
        import jax, jax.numpy as jnp
        import numpy as np
        TOPK = 4
        vecs = jnp.einsum('arh,bsh->bsar', A, x)
        arrows = jnp.linalg.norm(vecs, axis=-1)
        _, idx = jax.lax.top_k(arrows, TOPK)
        routes = jax.nn.one_hot(idx, arrows.shape[-1], dtype=x.dtype).sum(-2) / TOPK
        v = jnp.einsum('bsa,bsar->bsr', routes, vecs)
        delta = jnp.einsum('bsa,ajr,bsr->bsj', routes, B, v)
        base = jnp.einsum('bsh,jh->bsj', x, W) + bias
        return base + delta
    x = _layernorm(x + _L0_attn_ref(x, L0_attn_w_qkv, L0_attn_w_o), axis=-1)
    x = _layernorm(x + _L0_xattn_ref(x, ctx_2048, ctx_2048, L0_xattn_Wh, L0_xattn_wg_w, L0_xattn_wo_w, L0_xattn_gn_gamma, L0_xattn_gn_beta), axis=-1)
    x = _layernorm(x + _L0_ffn_ref(x, L0_ffn_A, L0_ffn_B, L0_ffn_W, L0_ffn_bias), axis=-1)
    return x

_drawn_inputs = setup_inputs


def setup_inputs(seed=0):
    import zlib

    import numpy as np

    out = dict(_drawn_inputs(seed))
    spreads = {'L0_xattn_gn_gamma': (1.0, 0.2), 'L0_xattn_gn_beta': (0.0, 0.1)}
    factors = {'L0_ffn_A': 5.373, 'L0_ffn_B': 4.538, 'L0_ffn_bias': 3.048}
    for name, (base, spread) in spreads.items():
        noise = np.random.default_rng([zlib.crc32(name.encode()), seed]).standard_normal(out[name].shape)
        drawn = base * np.exp(spread * noise) if base else spread * noise
        out[name] = jnp.asarray(drawn.astype(out[name].dtype))
    for name, factor in factors.items():
        out[name] = (out[name] * factor).astype(out[name].dtype)
    return out
```

```python
from contextlib import ExitStack

import concourse.bass as bass
from concourse import mybir

F32 = mybir.dt.float32
F32R = mybir.dt.float32r
BF16 = mybir.dt.bfloat16
U32 = mybir.dt.uint32
ALU = mybir.AluOpType
ACT = mybir.ActivationFunctionType
AX = mybir.AxisListType

P = 128
B, S, D = 4, 256, 256
KD = D // P
QT = S // P
NH, HD = 16, 16
XH = 2
EXP, RANK, TOPK = 64, 16, 4
ER = EXP * RANK
NEG = -3.0e38
HI = 3 * HD
HM = HI + 2
HB = 8
SG = 6

W_QK, W_V, W_O, W_H, W_G, W_O2, W_F = 0, 1024, 1536, 2048, 2304, 2816, 3328
W_N = 3840
FFN_TILES = B * QT


def ffn_tile(u):
    q = u // 2
    return 2 * (q % 2) + u % 2, q // 2


def plan():
    wide = [("qk", 0), ("qk", 1)] + [("s", 0, g) for g in range(SG)]
    narrow = [("v", 0), ("v", 1), ("mt", 0)]
    for i in range(B):
        if i + 2 < B:
            wide.append(("qk", i + 2))
            narrow.append(("v", i + 2))
        for g in range(SG):
            if i + 1 < B:
                wide.append(("s", i + 1, g))
            wide.append(("t", i, g))
            if i >= 1:
                narrow += {0: [("at", i - 1)], 1: [("wo", i - 1)], 3: [("xt", i - 1)],
                           4: [("gate", i - 1), ("xq", i - 1)]}.get(g, [])
        narrow += [("o", i, 0), ("o", i, 1)]
        if i + 1 < B:
            narrow.append(("mt", i + 1))
    L = B - 1
    wide += [("xk", 0), ("xk", 1), ("xv", 0), ("xv", 1)]
    narrow += [("at", L), ("wo", L), ("xt", L), ("gate", L), ("xq", L), ("sx", 0), ("sx", 1)]
    wide += [("ox", 0), ("ox", 1), ("ve", 0), ("ve", 1)]
    narrow += [("yt", 0), ("yt", 1), ("w2", 0), ("w2", 1), ("yt", 2), ("x2t", 0), ("yt", 3),
               ("w2", 2), ("w2", 3), ("x2t", 1), ("x2t", 2), ("x2t", 3)]
    for u in range(2, FFN_TILES + 3):
        if u < FFN_TILES:
            wide.append(("ve", u))
        if 0 <= u - 3 < FFN_TILES:
            narrow.append(("d", u - 3))
        if 0 <= u - 2 < FFN_TILES:
            wide.append(("zt", u - 2))
    return wide, narrow


WIDE, NARROW = plan()
WIDE_SLOTS, NARROW_SLOTS = 3, 2
SLOT = {k: n % WIDE_SLOTS for n, k in enumerate(WIDE)}
SLOT.update({k: n % NARROW_SLOTS for n, k in enumerate(NARROW)})
BEFORE = {k: WIDE[n - WIDE_SLOTS] for n, k in enumerate(WIDE) if n >= WIDE_SLOTS}
BEFORE.update({k: NARROW[n - NARROW_SLOTS] for n, k in enumerate(NARROW) if n >= NARROW_SLOTS})


def decoder_layer(nc, x, xT, cT, w, aT, bT, gam, bet, bias, decay, out):
    with ExitStack() as ctx:
        def sb(name, shape, dt=F32, stack=ctx):
            return stack.enter_context(nc.sbuf_tensor(name, shape, dt))

        def sem(name):
            return ctx.enter_context(nc.semaphore(name))

        ident = sb("ident", [P, P])
        ident_bf = sb("ident_bf", [P, P], BF16)
        causal = sb("causal", [P, P], BF16)
        iota = sb("iota", [P, EXP])
        neg_half = sb("neg_half", [P, 4])
        w_raw = sb("w_raw", [P, 4096])
        w_h = sb("w_h", [P, W_N], F32R)
        w_l = sb("w_l", [P, W_N], F32R)
        resid = sb("resid", [P, B, QT, D])
        act_raw = sb("act_raw", [P, KD, B * S])
        x1T_h = sb("x1T_h", [P, KD, S], F32R)
        x1T_l = sb("x1T_l", [P, KD, S], F32R)
        xq_h = sb("xq_h", [P, XH, B, S], F32R)
        xq_l = sb("xq_l", [P, XH, B, S], F32R)
        gate = sb("gate", [P, B, QT, D])
        pre = sb("pre", [P, 2, D])
        stats = sb("stats", [P, 4, 6])
        mv = sb("mv", [P, 4, 2])
        ve = sb("ve", [P, 4])
        rstd = sb("rstd", [P, 4])
        rden = sb("rden", [P, QT, NH], F32)
        attn = sb("attn", [P, QT, D], F32)
        aT_h = sb("aT_h", [P, KD, S], F32R)
        aT_l = sb("aT_l", [P, KD, S], F32R)
        att = ExitStack()
        xT_h = sb("xT_h", [P, KD, S], F32R, att)
        xT_l = sb("xT_l", [P, KD, S], F32R, att)
        qk_h = sb("qk_h", [P, 4, S], F32R, att)
        qk_l = sb("qk_l", [P, 4, S], F32R, att)
        qs = [sb(f"qs{i}", [HM, NH, S], F32R, att) for i in range(2)]
        ks = [sb(f"ks{i}", [64, NH, S], F32R, att) for i in range(2)]
        vs = [sb(f"vs{i}", [P, QT, NH, HD + 1], F32, att) for i in range(3)]
        probs = sb("probs", [P, SG, 1024], F32, att)
        nm = sb("nm", [P, QT, NH], F32, att)
        nm_hl = sb("nm_hl", [P, QT, 2, NH], F32R, att)
        nmT = sb("nmT", [2 * NH, S], F32R, att)
        att.close()
        ea_h = sb("ea_h", [P, KD, ER], F32R)
        ea_l = sb("ea_l", [P, KD, ER], F32R)
        eb_h = sb("eb_h", [P, ER // P, D], F32R)
        eb_l = sb("eb_l", [P, ER // P, D], F32R)
        gam_b = sb("gam_b", [P, D])
        bet_b = sb("bet_b", [P, D])
        bias_b = sb("bias_b", [P, D])
        y = sb("y", [P, QT, B, D])
        yT_h = sb("yT_h", [P, KD, S], F32R)
        yT_l = sb("yT_l", [P, KD, S], F32R)
        ret = ExitStack()
        cT_h = sb("cT_h", [P, KD, B * S], F32R, ret)
        cT_l = sb("cT_l", [P, KD, B * S], F32R, ret)
        xk_h = sb("xk_h", [P, XH, B * S], F32R, ret)
        xk_l = sb("xk_l", [P, XH, B * S], F32R, ret)
        xv_h = sb("xv_h", [P, QT, XH, B, P], F32R, ret)
        xv_l = sb("xv_l", [P, QT, XH, B, P], F32R, ret)
        dec = sb("dec", [P, XH, 384], F32, ret)
        mag = sb("mag", [P, XH, 384], F32, ret)
        rA_h = sb("rA_h", [P, XH, 384], F32R, ret)
        rA_l = sb("rA_l", [P, XH, 384], F32R, ret)
        ones_f = sb("ones_f", [P, P], F32, ret)
        ones_r = sb("ones_r", [P, P], F32R, ret)
        ret.close()
        x2T_h = sb("x2T_h", [P, 4, KD, S], F32R)
        x2T_l = sb("x2T_l", [P, 4, KD, S], F32R)
        sq = sb("sq", [P, ER])
        vc = [sb(f"vc{i}", [P, ER]) for i in range(2)]
        n2 = sb("n2", [P, EXP])
        top = sb("top", [P, 8])
        idx = sb("idx", [P, 8], U32)
        idxf = sb("idxf", [P, 8])
        route = [sb(f"route{i}", [P, EXP]) for i in range(2)]
        vr = [sb(f"vr{i}", [P, RANK]) for i in range(2)]
        z = [sb(f"z{i}", [P, ER]) for i in range(2)]
        zT_h = sb("zT_h", [P, ER // P, P], F32R)
        zT_l = sb("zT_l", [P, ER // P, P], F32R)
        res = [sb(f"res{i}", [P, D]) for i in range(2)]

        wide_ps = [ctx.enter_context(nc.psum_tensor(f"wide{i}", [P, 1024], F32)) for i in range(WIDE_SLOTS)]
        narrow_ps = [ctx.enter_context(nc.psum_tensor(f"narrow{i}", [P, 512], F32)) for i in range(NARROW_SLOTS)]

        def wide(*key):
            return wide_ps[SLOT[key]]

        def narrow(*key):
            return narrow_ps[SLOT[key]]

        ld_x, ld_w, ld_c, ld_res, ld_a, ld_b, ld_vec, ld_dec = (sem(n) for n in (
            "ld_x", "ld_w", "ld_c", "ld_res", "ld_a", "ld_b", "ld_vec", "ld_dec"))
        stacked = [sem(f"stacked{i}") for i in range(2)]
        nm_stacked = sem("nm_stacked")
        stored = [sem(f"stored{i}") for i in range(2)]
        pool_const = sem("pool_const")
        iota_ready = sem("iota_ready")
        ones_ready = sem("ones_ready")
        wqk_h, wqk_l, wv_h, wv_l, wr_h, wr_l = (sem(n) for n in ("wqk_hi", "wqk_lo", "wv_hi", "wv_lo", "wr_hi", "wr_lo"))
        xT_hi, xT_lo, cT_hi, cT_lo = (sem(n) for n in ("xT_hi", "xT_lo", "cT_hi", "cT_lo"))
        ea_hi, ea_lo, eb_hi, eb_lo = (sem(n) for n in ("ea_hi", "ea_lo", "eb_hi", "eb_lo"))
        kinds = ("qk", "v", "s", "mt", "t", "o", "at", "wo", "xt", "gate", "xq", "xk", "xv", "sx", "ox", "yt",
                 "w2", "x2t", "ve", "zt", "d")
        full = {k: sem("pe_" + k) for k in kinds}
        hi = {k: sem(k + "_hi") for k in ("qk", "at", "xt", "xq", "xk", "xv", "yt", "x2t", "zt")}
        lo = {k: sem(k + "_lo") for k in ("qk", "at", "xt", "xq", "xk", "xv", "yt", "x2t", "zt")}
        v_copied, maxed, nm_hi, nm_lo, nmT_copied = (sem(n) for n in ("v_copied", "maxed", "nm_hi", "nm_lo", "nmT_copied"))
        exped, masked, rden_done, attn_done, gated = (sem(n) for n in ("exped", "masked", "rden_done", "attn_done", "gated"))
        added, stat_done, mv_done, ve_done, rstd_done, normed = (sem(n) for n in (
            "added", "stat_done", "mv_done", "ve_done", "rstd_done", "normed"))
        abs_done, decayed, rA_hi, rA_lo = (sem(n) for n in ("abs_done", "decayed", "rA_hi", "rA_lo"))
        y_gam, y_bet, y_done = (sem(n) for n in ("y_gam", "y_bet", "y_done"))
        squared, vc_done, n2_done, top_done, idx_done, idxf_done, route_step = (sem(n) for n in (
            "squared", "vc_done", "n2_done", "top_done", "idx_done", "idxf_done", "route_step"))
        picked, v_done, z_done, biased = (sem(n) for n in ("picked", "v_done", "z_done", "biased"))

        def released(key):
            k, n = key[0], key[1:]
            if k in ("qk", "at", "xt", "xq", "xk", "yt", "x2t", "zt"):
                return lo[k], n[0] + 1
            return {
                "xv": lambda: (lo["xv"], 2 * n[0] + 2),
                "v": lambda: (v_copied, n[0] + 1),
                "s": lambda: (maxed, SG * n[0] + n[1] + 1),
                "mt": lambda: (nmT_copied, n[0] + 1),
                "t": lambda: (exped, SG * n[0] + n[1] + 1),
                "o": lambda: (attn_done, QT * n[0] + n[1] + 1),
                "wo": lambda: (added, n[0] + 1),
                "gate": lambda: (gated, n[0] + 1),
                "sx": lambda: (abs_done, n[0] + 1),
                "ox": lambda: (y_gam, B * n[0] + B),
                "w2": lambda: (added, B + n[0] + 1),
                "ve": lambda: (vc_done, n[0] + 1),
                "d": lambda: (added, B + 4 + n[0] + 1),
            }[k]()

        block = ctx.enter_context(nc.Block())

        @block.sync
        def _(sp):
            sp.dma_start(act_raw[:], xT).then_inc(ld_x, 16)
            sp.dma_start(resid[:], x).then_inc(ld_res, 16)

            def stack_scores(b):
                sp.wait_ge(hi["qk"], b + 1)
                sp.wait_ge(lo["qk"], b + 1)
                if b < 2:
                    sp.wait_ge(ones_ready, 2)
                else:
                    sp.wait_ge(full["t"], SG * (b - 1))
                for t, n, (q, k) in ((0, 0, (qk_h, qk_h)), (1, 1, (qk_h, qk_l)), (2, 2, (qk_l, qk_h))):
                    rows = slice(HD * n, HD * (n + 1))
                    sp.dma_start(qs[b % 2][rows].bitcast(F32), q[:, 0:2, :].bitcast(F32)).then_inc(stacked[b % 2], 16)
                    sp.dma_start(ks[b % 2][rows].bitcast(F32), k[:, 2:4, :].bitcast(F32)).then_inc(stacked[b % 2], 16)

            def stack_max(b):
                sp.wait_ge(nmT_copied, b + 1)
                if b >= 2:
                    sp.wait_ge(full["t"], SG * (b - 1))
                sp.dma_start(qs[b % 2][HI:HM].bitcast(F32), nmT[:].bitcast(F32)).then_inc(nm_stacked, 16)

            stack_scores(0)
            stack_scores(1)
            stack_max(0)
            for i in range(B):
                if i == 0:
                    sp.wait_ge(xT_lo, B)
                    sp.wait_ge(xT_hi, B)
                    sp.dma_start(act_raw[:], cT).then_inc(ld_c, 16)
                if i + 2 < B:
                    stack_scores(i + 2)
                if i + 1 < B:
                    stack_max(i + 1)
            sp.wait_ge(full["o"], 2 * B)
            sp.dma_start(gam_b[:], gam).then_inc(ld_vec, 16)
            sp.dma_start(bet_b[:], bet).then_inc(ld_vec, 16)
            sp.dma_start(bias_b[:], bias).then_inc(ld_vec, 16)
            sp.dma_start(dec[:], decay).then_inc(ld_dec, 16)
            for u in range(FFN_TILES):
                b, t = ffn_tile(u)
                sp.wait_ge(normed, 2 * B + 8 + u + 1)
                sp.dma_start(out[:, b, t, :], res[u % 2][:]).then_inc(stored[u % 2], 16)
            sp.wait_ge(stored[0], 16 * (FFN_TILES // 2))
            sp.wait_ge(stored[1], 16 * (FFN_TILES // 2))

        @block.scalar
        def _(act):
            act.dma_start(w_raw[:, 0:W_N], w).then_inc(ld_w, 16)
            act.wait_ge(ld_x, 16)
            act.activation(xT_h[:], act_raw[:, :, 0:S], ACT.Copy).then_inc(xT_hi, 1)
            act.wait_ge(ld_w, 16)
            act.activation(w_h[:, W_QK:W_V], w_raw[:, W_QK:W_V], ACT.Copy).then_inc(wqk_h, 1)
            act.activation(w_h[:, W_V:W_O], w_raw[:, W_V:W_O], ACT.Copy).then_inc(wv_h, 1)

            def qk_hi(b):
                act.wait_ge(full["qk"], b + 1)
                if b >= 1:
                    act.wait_ge(stacked[(b - 1) % 2], 96 * ((b - 1) // 2 + 1))
                act.activation(qk_h[:], wide("qk", b)[:].rearrange("p (m s) -> p m s", m=4), ACT.Copy)\
                   .then_inc(hi["qk"], 1)

            def v_copy(b):
                act.wait_ge(full["v"], b + 1)
                if b < 3:
                    act.wait_ge(ones_ready, 2 + b + 1)
                else:
                    act.wait_ge(full["o"], 2 * (b - 2))
                act.activation(vs[b % 3][:].rearrange("p t h e -> p (t h) e")[:, :, 0:HD],
                               narrow("v", b)[:].rearrange("p (n d) -> p n d", d=HD), ACT.Copy)\
                   .then_inc(v_copied, 1)

            def nmT_copy(b):
                act.wait_ge(full["mt"], b + 1)
                if b >= 1:
                    act.wait_ge(nm_stacked, 16 * b)
                act.activation(nmT[:], narrow("mt", b)[0:2 * NH, 0:S], ACT.Copy).then_inc(nmT_copied, 1)

            def split_hi(kind, n, dst, src):
                act.wait_ge(full[kind], n + 1)
                act.activation(dst, src, ACT.Copy).then_inc(hi[kind], 1)

            def exp_group(b, g):
                act.wait_ge(full["t"], SG * b + g + 1)
                if b >= 1:
                    act.wait_ge(full["o"], 2 * b)
                act.activation(probs[:, g, :], wide("t", b, g)[:], ACT.Exp, scale=HD ** -0.5).then_inc(exped, 1)

            def tail(b, g):
                if g == 0:
                    if b >= 1:
                        act.wait_ge(full["wo"], b)
                    split_hi("at", b, aT_h[:].rearrange("p k s -> p (k s)"), narrow("at", b)[:])
                if g == 3:
                    if b >= 1:
                        act.wait_ge(full["xq"], b)
                    split_hi("xt", b, x1T_h[:].rearrange("p k s -> p (k s)"), narrow("xt", b)[:])
                if g == 4:
                    act.wait_ge(full["gate"], b + 1)
                    act.activation(gate[:, b].rearrange("p t d -> p (t d)"), narrow("gate", b)[:], ACT.Relu)\
                       .then_inc(gated, 1)
                    split_hi("xq", b, xq_h[:, :, b, :], narrow("xq", b)[:].rearrange("p (h s) -> p h s", h=XH))

            for b in range(2):
                qk_hi(b)
                v_copy(b)
            nmT_copy(0)
            for i in range(B):
                if i + 2 < B:
                    qk_hi(i + 2)
                    v_copy(i + 2)
                for g in range(SG):
                    exp_group(i, g)
                    if i >= 1:
                        tail(i - 1, g)
                if i + 1 < B:
                    nmT_copy(i + 1)
            act.wait_ge(ld_c, 16)
            act.wait_ge(full["o"], 2 * B)
            for k in range(KD):
                act.activation(cT_h[:, k], act_raw[:, k], ACT.Copy).then_inc(cT_hi, 1)

            def keys_hi(c):
                split_hi("xk", c, xk_h[:, :, c * 512:c * 512 + 512], wide("xk", c)[:].rearrange("p (h s) -> p h s", h=XH))

            def values_hi(c):
                act.wait_ge(full["xv"], c + 1)
                for n in range(2):
                    act.activation(xv_h[:, :, :, 2 * c + n, :],
                                   wide("xv", c)[:, n * 512:n * 512 + 512].rearrange("p (t h e) -> p t h e", t=QT, h=XH),
                                   ACT.Copy).then_inc(hi["xv"], 1)

            keys_hi(0)
            keys_hi(1)
            tail(B - 1, 0)
            values_hi(0)
            values_hi(1)
            tail(B - 1, 3)
            tail(B - 1, 4)
            for h in range(XH):
                act.wait_ge(full["sx"], h + 1)
                act.activation(mag[:, h], narrow("sx", h)[:, 0:384], ACT.Abs).then_inc(abs_done, 1)

            def yT_split(q):
                if q >= 1:
                    act.wait_ge(full["w2"], q)
                split_hi("yt", q, yT_h[:].rearrange("p k s -> p (k s)"), narrow("yt", q)[:])

            def x2T_split(q):
                act.wait_ge(full["ox"], 2)
                split_hi("x2t", q, x2T_h[:, q].rearrange("p k s -> p (k s)"), narrow("x2t", q)[:])

            def square(u):
                act.wait_ge(full["ve"], u + 1)
                if u >= 1:
                    act.wait_ge(n2_done, u)
                act.activation(sq[:], wide("ve", u)[:], ACT.Square).then_inc(squared, 1)
                if u >= 2:
                    act.wait_ge(picked, u - 1)
                    act.wait_ge(v_done, u - 1)
                act.activation(vc[u % 2][:], wide("ve", u)[:], ACT.Copy, scale=1.0 / TOPK ** 2).then_inc(vc_done, 1)

            def zT_split(u):
                if u >= 1:
                    act.wait_ge(full["d"], u)
                split_hi("zt", u, zT_h[:].rearrange("p k s -> p (k s)"), wide("zt", u)[:])

            yT_split(0)
            yT_split(1)
            yT_split(2)
            x2T_split(0)
            yT_split(3)
            square(0)
            x2T_split(1)
            square(1)
            x2T_split(2)
            x2T_split(3)
            for u in range(2, FFN_TILES + 2):
                if u < FFN_TILES:
                    square(u)
                if u - 2 < FFN_TILES:
                    zT_split(u - 2)

        @block.gpsimd
        def _(pool):
            pool.memset(ident[:], 0.0).then_inc(pool_const, 1)
            pool.memset(causal[:], 0.0).then_inc(pool_const, 1)
            pool.memset(neg_half[:], -0.5).then_inc(pool_const, 1)
            pool.wait_ge(pool_const, 3)
            pool.affine_select(out=ident[:], in_=ident[:], pattern=[[-1, P]], compare_op=ALU.not_equal, fill=1.0,
                               base=0, channel_multiplier=1).then_inc(pool_const, 1)
            pool.affine_select(out=causal[:], in_=causal[:], pattern=[[-1, P]], compare_op=ALU.is_ge, fill=NEG,
                               base=0, channel_multiplier=1).then_inc(pool_const, 1)
            pool.wait_ge(pool_const, 5)
            pool.tensor_copy(ident_bf[:], ident[:]).then_inc(pool_const, 1)
            pool.wait_ge(pool_const, 6)
            for i in range(2):
                pool.memset(ks[i][32:64].bitcast(F32), 1.0).then_inc(ones_ready, 1)
            pool.wait_ge(ones_ready, 2)
            for i in range(3):
                pool.memset(vs[i][:].rearrange("p t h e -> p (t h) e")[:, :, HD:HD + 1], 1.0).then_inc(ones_ready, 1)

            def split(dst_h, dst_l, src, sem_h, sem_l, n):
                pool.tensor_copy(dst_h, src).then_inc(sem_h, 1)
                pool.wait_ge(sem_h, n)
                pool.tensor_tensor(dst_l, src, dst_h.bitcast(F32), ALU.subtract).then_inc(sem_l, 1)

            pool.wait_ge(ld_w, 16)
            pool.wait_ge(wv_h, 1)
            pool.tensor_tensor(w_l[:, W_V:W_O], w_raw[:, W_V:W_O], w_h[:, W_V:W_O].bitcast(F32), ALU.subtract)\
                .then_inc(wv_l, 1)

            def split_x(b):
                pool.wait_ge(full["qk"], b)
                pool.wait_ge(full["v"], b)
                pool.wait_ge(xT_hi, b)
                split(xT_h[:], xT_l[:], act_raw[:, :, b * S:(b + 1) * S], xT_hi, xT_lo, b + 1)

            split_x(1)
            split_x(2)
            for n, (a, z_) in enumerate(((W_O, W_H), (W_H, W_G), (W_G, W_O2), (W_O2, W_F), (W_F, W_N))):
                split(w_h[:, a:z_], w_l[:, a:z_], w_raw[:, a:z_], wr_h, wr_l, n + 1)
            pool.iota(iota[:], pattern=[[1, EXP]], base=0, channel_multiplier=0,
                      allow_small_or_imprecise_dtypes=True).then_inc(iota_ready, 1)
            pool.wait_ge(wqk_l, 1)
            pool.wait_ge(wr_l, 5)
            pool.dma_start(w_raw[:, 0:2048], aT).then_inc(ld_a, 16)
            pool.dma_start(w_raw[:, 2048:4096], bT).then_inc(ld_b, 16)

            def cut(b, g):
                pool.wait_ge(exped, SG * b + g + 1)
                v = probs[:, g, :].rearrange("p (h q) -> p h q", q=S if g < 4 else P)[:, :, 0:P]
                pool.affine_select(out=v, in_=v, pattern=[[0, 4 if g < 4 else 8], [1, P]], compare_op=ALU.is_ge,
                                   fill=0.0, base=0, channel_multiplier=-1).then_inc(masked, 1)

            powers = [0]

            def power(n):
                powers[0] += 1
                pool.wait_ge(ve_done, powers[0])
                pool.tensor_tensor(rstd[:, 0:n], ve[:, 0:n], neg_half[:, 0:n], ALU.pow).then_inc(rstd_done, 1)

            for i in range(B):
                for g in range(SG):
                    if i == 1 and g == 0:
                        split_x(3)
                    if i == 0 and g == 0:
                        pass
                    cut(i, g)
                    if i >= 1 and g == 2:
                        power(2)
            pool.wait_ge(ld_c, 16)
            pool.wait_ge(full["o"], 2 * B)
            pool.wait_ge(cT_hi, 1)
            pool.tensor_tensor(cT_l[:, 0], act_raw[:, 0], cT_h[:, 0].bitcast(F32), ALU.subtract).then_inc(cT_lo, 1)
            pool.memset(ones_f[:], 1.0).then_inc(ones_ready, 1)
            pool.wait_ge(ones_ready, 6)
            pool.tensor_copy(ones_r[:], ones_f[:]).then_inc(ones_ready, 1)
            power(2)
            pool.wait_ge(ld_a, 16)
            for n in range(KD):
                split(ea_h[:, n], ea_l[:, n], w_raw[:, n * ER:(n + 1) * ER], ea_hi, ea_lo, n + 1)
            pool.wait_ge(ld_b, 16)
            power(4)
            split(eb_h[:, 0:4], eb_l[:, 0:4], w_raw[:, 2048:3072].rearrange("p (k j) -> p k j", j=D), eb_hi, eb_lo, 1)
            power(4)
            split(eb_h[:, 4:8], eb_l[:, 4:8], w_raw[:, 3072:4096].rearrange("p (k j) -> p k j", j=D), eb_hi, eb_lo, 2)

            def add_bias(q):
                pool.wait_ge(full["x2t"], q + 1)
                if q == 0:
                    pool.wait_ge(ld_vec, 48)
                for j in range(2):
                    b, t = ffn_tile(2 * q + j)
                    pool.tensor_tensor(resid[:, b, t], resid[:, b, t], bias_b[:], ALU.add).then_inc(biased, 1)

            def pick(u):
                pool.wait_ge(route_step, 4 * u + 4)
                pool.wait_ge(vc_done, u + 1)
                v = vc[u % 2][:].rearrange("p (a r) -> p a r", r=RANK)
                pool.tensor_tensor(v, v, route[u % 2][:].unsqueeze(2).broadcast_to([P, EXP, RANK]), ALU.mult)\
                    .then_inc(picked, 1)

            def spread(u):
                pool.wait_ge(v_done, u + 1)
                if u >= 2:
                    pool.wait_ge(full["zt"], u - 1)
                pool.tensor_tensor(z[u % 2][:].rearrange("p (a r) -> p a r", r=RANK),
                                   route[u % 2][:].unsqueeze(2).broadcast_to([P, EXP, RANK]),
                                   vr[u % 2][:].unsqueeze(1).broadcast_to([P, EXP, RANK]), ALU.mult).then_inc(z_done, 1)

            power(2)
            power(2)
            power(2)
            power(2)
            add_bias(0)
            add_bias(1)
            pick(0)
            add_bias(2)
            add_bias(3)
            for u in range(FFN_TILES):
                spread(u)
                if u + 1 < FFN_TILES:
                    pick(u + 1)
                if u >= 2:
                    power(1)
            power(1)
            power(1)

        @block.vector
        def _(dve):
            count = {"added": 0, "stat": 0, "mv": 0, "ve": 0, "normed": 0}

            def low(dst, src, high, s, n_hi=None):
                dve.tensor_tensor(dst, src, high.bitcast(F32), ALU.subtract).then_inc(s, 1)

            dve.wait_ge(xT_hi, 1)
            low(xT_l[:], act_raw[:, :, 0:S], xT_h[:], xT_lo)
            dve.wait_ge(wqk_h, 1)
            low(w_l[:, W_QK:W_V], w_raw[:, W_QK:W_V], w_h[:, W_QK:W_V], wqk_l)

            def qk_lo(b):
                dve.wait_ge(hi["qk"], b + 1)
                low(qk_l[:], wide("qk", b)[:].rearrange("p (m s) -> p m s", m=4), qk_h[:], lo["qk"])

            def row_max(b, g):
                dve.wait_ge(full["s"], SG * b + g + 1)
                if b >= 1 and g == 0:
                    dve.wait_ge(full["mt"], b)
                if g < 2:
                    dst, keys = nm[:, 0, 8 * g:8 * g + 8], P
                else:
                    dst, keys = nm[:, 1, 4 * (g - 2):4 * (g - 2) + 4], S
                dve.tensor_reduce(dst, wide("s", b, g)[:].rearrange("p (h k) -> p h k", k=keys), AX.X, ALU.max,
                                  negate=True).then_inc(maxed, 1)

            def split_max(b):
                dve.wait_ge(maxed, SG * (b + 1))
                dve.tensor_copy(nm_hl[:, :, 0, :], nm[:]).then_inc(nm_hi, 1)
                dve.wait_ge(nm_hi, b + 1)
                low(nm_hl[:, :, 1, :], nm[:], nm_hl[:, :, 0, :], nm_lo)

            def normalise_attn(b):
                if b >= 1:
                    dve.wait_ge(full["at"], b)
                for t in range(QT):
                    dve.wait_ge(full["o"], 2 * b + t + 1)
                    o = narrow("o", b, t)[:, 0:NH * (HD + 1)].rearrange("p (h e) -> p h e", e=HD + 1)
                    dve.reciprocal(rden[:, t, :], o[:, :, HD]).then_inc(rden_done, 1)
                    dve.wait_ge(rden_done, 2 * b + t + 1)
                    dve.tensor_tensor(attn[:, t].rearrange("p (h d) -> p h d", d=HD), o[:, :, 0:HD],
                                      rden[:, t, :].unsqueeze(2).broadcast_to([P, NH, HD]), ALU.mult)\
                       .then_inc(attn_done, 1)

            def statistics(tiles, eps):
                n = len(tiles)
                for j, v in enumerate(tiles):
                    dve.bn_stats(stats[:, j], v).then_inc(stat_done, 1)
                count["stat"] += n
                for j in range(n):
                    if j == 0:
                        dve.wait_ge(stat_done, count["stat"])
                    dve.bn_aggr(mv[:, j], stats[:, j]).then_inc(mv_done, 1)
                count["mv"] += n
                dve.wait_ge(mv_done, count["mv"])
                dve.tensor_scalar(ve[:, 0:n], mv[:, 0:n, 1], eps, None, ALU.add).then_inc(ve_done, 1)
                count["ve"] += 1

            def add_norm(psum, old, news):
                n = len(news)
                if count["normed"]:
                    dve.wait_ge(normed, count["normed"])
                dve.tensor_tensor(pre[:, 0:n], psum, old, ALU.add).then_inc(added, 1)
                count["added"] += 1
                dve.wait_ge(added, count["added"])
                statistics([pre[:, j] for j in range(n)], 1e-5)
                dve.wait_ge(rstd_done, count["ve"])
                for j, v in enumerate(news):
                    dve.tensor_scalar(v, pre[:, j], mv[:, j, 0:1], rstd[:, j:j + 1], ALU.subtract, ALU.mult)\
                       .then_inc(normed, 1)
                count["normed"] += n

            def split_lo(kind, n, dst, src, high):
                dve.wait_ge(hi[kind], n + 1)
                low(dst, src, high, lo[kind])

            def tail(b, g):
                if g == 0:
                    split_lo("at", b, aT_l[:].rearrange("p k s -> p (k s)"), narrow("at", b)[:],
                             aT_h[:].rearrange("p k s -> p (k s)"))
                if g == 2:
                    dve.wait_ge(full["wo"], b + 1)
                    if b == 0:
                        dve.wait_ge(ld_res, 16)
                    add_norm(narrow("wo", b)[:].rearrange("p (t d) -> p t d", t=QT), resid[:, b],
                             [resid[:, b, t] for t in range(QT)])
                if g == 3:
                    split_lo("xt", b, x1T_l[:].rearrange("p k s -> p (k s)"), narrow("xt", b)[:],
                             x1T_h[:].rearrange("p k s -> p (k s)"))
                if g == 5:
                    split_lo("xq", b, xq_l[:, :, b, :], narrow("xq", b)[:].rearrange("p (h s) -> p h s", h=XH),
                             xq_h[:, :, b, :])

            for b in range(2):
                qk_lo(b)
            for g in range(SG):
                row_max(0, g)
            split_max(0)
            for i in range(B):
                if i + 2 < B:
                    qk_lo(i + 2)
                for g in range(SG):
                    if i + 1 < B:
                        row_max(i + 1, g)
                    if i >= 1:
                        tail(i - 1, g)
                if i + 1 < B:
                    split_max(i + 1)
                normalise_attn(i)
            dve.wait_ge(cT_hi, 2)
            low(cT_l[:, 1], act_raw[:, 1], cT_h[:, 1], cT_lo)

            def keys_lo(c):
                v = slice(c * 512, c * 512 + 512)
                split_lo("xk", c, xk_l[:, :, v], wide("xk", c)[:].rearrange("p (h s) -> p h s", h=XH), xk_h[:, :, v])

            def values_lo(c):
                for n in range(2):
                    b = 2 * c + n
                    split_lo("xv", b, xv_l[:, :, :, b, :],
                             wide("xv", c)[:, n * 512:n * 512 + 512].rearrange("p (t h e) -> p t h e", t=QT, h=XH),
                             xv_h[:, :, :, b, :])

            keys_lo(0)
            keys_lo(1)
            tail(B - 1, 0)
            values_lo(0)
            tail(B - 1, 2)
            values_lo(1)
            tail(B - 1, 3)
            tail(B - 1, 5)
            dve.wait_ge(ld_dec, 16)
            for h in range(XH):
                dve.wait_ge(abs_done, h + 1)
                dve.tensor_tensor(mag[:, h], mag[:, h], dec[:, h], ALU.mult).then_inc(decayed, 1)
                dve.wait_ge(decayed, h + 1)
                dve.tensor_scalar(rA_h[:, h], mag[:, h], 1.0, None, ALU.max).then_inc(rA_hi, 1)
                dve.wait_ge(rA_hi, h + 1)
                dve.scalar_tensor_tensor(out=rA_l[:, h], in0=mag[:, h], scalar=1.0, in1=rA_h[:, h].bitcast(F32),
                                         op0=ALU.max, op1=ALU.subtract).then_inc(rA_lo, 1)
            dve.wait_ge(ld_vec, 48)
            dve.wait_ge(gated, B)

            def group_norm(t):
                dve.wait_ge(full["ox"], t + 1)
                dve.wait_ge(normed, count["normed"])
                o = wide("ox", t)[:].rearrange("p (h b e) -> p b h e", h=XH, b=B)
                if t >= 1:
                    dve.wait_ge(y_bet, B * t)
                statistics([o[:, b] for b in range(B)], 1e-3)
                g3 = gam_b[:].rearrange("p (h e) -> p h e", h=XH)
                for b in range(B):
                    dve.scalar_tensor_tensor(out=y[:, t, b].rearrange("p (h e) -> p h e", h=XH), in0=o[:, b],
                                             scalar=mv[:, b, 0:1], in1=g3, op0=ALU.subtract, op1=ALU.mult)\
                       .then_inc(y_gam, 1)
                dve.wait_ge(rstd_done, count["ve"])
                dve.wait_ge(y_gam, B * t + B)
                for b in range(B):
                    dve.scalar_tensor_tensor(out=y[:, t, b], in0=y[:, t, b], scalar=rstd[:, b:b + 1], in1=bet_b[:],
                                             op0=ALU.mult, op1=ALU.add).then_inc(y_bet, 1)
                dve.wait_ge(y_bet, B * t + B)
                for b in range(B):
                    dve.tensor_tensor(y[:, t, b], y[:, t, b], gate[:, b, t], ALU.mult).then_inc(y_done, 1)

            def yT_split(q):
                split_lo("yt", q, yT_l[:].rearrange("p k s -> p (k s)"), narrow("yt", q)[:],
                         yT_h[:].rearrange("p k s -> p (k s)"))

            def second_norm(q):
                t, b0 = q // 2, 2 * (q % 2)
                dve.wait_ge(full["w2"], q + 1)
                dve.wait_ge(y_bet, B * (t + 1))
                add_norm(narrow("w2", q)[:].rearrange("p (t d) -> p t d", t=2), resid[:, b0:b0 + 2, t],
                         [resid[:, b0 + j, t] for j in range(2)])

            def x2T_split(q):
                split_lo("x2t", q, x2T_l[:, q].rearrange("p k s -> p (k s)"), narrow("x2t", q)[:],
                         x2T_h[:, q].rearrange("p k s -> p (k s)"))

            def route_tile(u):
                dve.wait_ge(squared, u + 1)
                dve.tensor_reduce(n2[:], sq[:].rearrange("p (a r) -> p a r", r=RANK), AX.X, ALU.add).then_inc(n2_done, 1)
                dve.wait_ge(n2_done, u + 1)
                dve.max(top[:], n2[:]).then_inc(top_done, 1)
                dve.wait_ge(top_done, u + 1)
                dve.max_index(idx[:], top[:], n2[:]).then_inc(idx_done, 1)
                dve.wait_ge(idx_done, u + 1)
                dve.tensor_copy(idxf[:], idx[:]).then_inc(idxf_done, 1)
                dve.wait_ge(idxf_done, u + 1)
                if u >= 2:
                    dve.wait_ge(z_done, u - 1)
                r = route[u % 2][:]
                dve.tensor_scalar(r, iota[:], idxf[:, 0:1], None, ALU.is_equal).then_inc(route_step, 1)
                for j in range(1, TOPK):
                    dve.wait_ge(route_step, TOPK * u + j)
                    dve.scalar_tensor_tensor(out=r, in0=iota[:], scalar=idxf[:, j:j + 1], in1=r, op0=ALU.is_equal,
                                             op1=ALU.add).then_inc(route_step, 1)

            def sum_picked(u):
                dve.wait_ge(picked, u + 1)
                if u >= 2:
                    dve.wait_ge(z_done, u - 1)
                dve.tensor_reduce(vr[u % 2][:], vc[u % 2][:].rearrange("p (a r) -> p r a", r=RANK), AX.X, ALU.add)\
                   .then_inc(v_done, 1)

            def zT_split(u):
                split_lo("zt", u, zT_l[:].rearrange("p k s -> p (k s)"), wide("zt", u)[:],
                         zT_h[:].rearrange("p k s -> p (k s)"))

            def last_norm(u):
                b, t = ffn_tile(u)
                dve.wait_ge(full["d"], u + 1)
                dve.wait_ge(biased, u + 1)
                if u >= 2:
                    dve.wait_ge(stored[u % 2], 16 * (u // 2))
                add_norm(narrow("d", u)[:, 0:D].unsqueeze(1), resid[:, b, t:t + 1], [res[u % 2][:]])

            group_norm(0)
            yT_split(0)
            group_norm(1)
            yT_split(1)
            second_norm(0)
            second_norm(1)
            yT_split(2)
            x2T_split(0)
            yT_split(3)
            second_norm(2)
            dve.wait_ge(iota_ready, 1)
            route_tile(0)
            second_norm(3)
            x2T_split(1)
            route_tile(1)
            x2T_split(2)
            x2T_split(3)
            sum_picked(0)
            for u in range(2, FFN_TILES + 3):
                if u < FFN_TILES:
                    route_tile(u)
                if 0 <= u - 1 < FFN_TILES:
                    sum_picked(u - 1)
                if 0 <= u - 2 < FFN_TILES:
                    zT_split(u - 2)
                if 0 <= u - 3 < FFN_TILES:
                    last_norm(u - 3)

        @block.tensor
        def _(pe):
            def take(*key):
                if key in BEFORE:
                    pe.wait_ge(*released(BEFORE[key]))

            def three(dst, wh, wl, xh, xl, start, stop):
                pe.matmul(dst, wh, xh, start=start, stop=False)
                pe.matmul(dst, wh, xl, start=False, stop=False)
                return pe.matmul(dst, wl, xh, start=False, stop=stop)

            def project_qk(b):
                take("qk", b)
                pe.wait_ge(xT_hi, b + 1)
                pe.wait_ge(xT_lo, b + 1)
                if b == 0:
                    pe.wait_ge(wqk_h, 1)
                    pe.wait_ge(wqk_l, 1)
                for m in range(4):
                    for k in range(KD):
                        c = W_QK + k * 512 + m * P
                        mm = three(wide("qk", b)[:, m * S:(m + 1) * S], w_h[:, c:c + P], w_l[:, c:c + P],
                                   xT_h[:, k], xT_l[:, k], k == 0, k == KD - 1)
                mm.then_inc(full["qk"], 1)

            def project_v(b):
                take("v", b)
                if b == 0:
                    pe.wait_ge(wv_h, 1)
                    pe.wait_ge(wv_l, 1)
                for t in range(QT):
                    for k in range(KD):
                        c = W_V + k * D
                        mm = three(narrow("v", b)[:, t * D:(t + 1) * D], xT_h[:, k, t * P:(t + 1) * P],
                                   xT_l[:, k, t * P:(t + 1) * P], w_h[:, c:c + D], w_l[:, c:c + D], k == 0, k == KD - 1)
                mm.then_inc(full["v"], 1)

            def scores(b, g):
                take("s", b, g)
                if g == 0:
                    pe.wait_ge(stacked[b % 2], 96 * (b // 2 + 1))
                if b == 0 and g == 0:
                    pe.wait_ge(pool_const, 6)
                q, k = qs[b % 2], ks[b % 2]
                t, heads, keys = (0, range(8 * g, 8 * g + 8), P) if g < 2 else (1, range(4 * g - 8, 4 * g - 4), S)
                for n, h in enumerate(heads):
                    dst = wide("s", b, g)[:, n * keys:(n + 1) * keys]
                    pe.matmul(dst, q[0:HI, h, t * P:(t + 1) * P], k[0:HI, h, 0:keys], start=True, stop=False)
                    mm = pe.matmul(dst[:, keys - P:keys], ident_bf[:], causal[:], start=False, stop=True)
                mm.then_inc(full["s"], 1)

            def max_rows(b):
                take("mt", b)
                pe.wait_ge(nm_lo, b + 1)
                for t in range(QT):
                    mm = pe.transpose(narrow("mt", b)[0:2 * NH, t * P:(t + 1) * P],
                                      nm_hl[:, t].rearrange("p a h -> p (a h)").bitcast(F32), ident[:])
                mm.then_inc(full["mt"], 1)

            def scores_T(b, g):
                take("t", b, g)
                if g == 0:
                    pe.wait_ge(nm_stacked, 16 * (b + 1))
                q, k = qs[b % 2], ks[b % 2]
                kt, heads, q0 = (0, range(4 * g, 4 * g + 4), 0) if g < 4 else (1, range(8 * g - 32, 8 * g - 24), P)
                for n, h in enumerate(heads):
                    mm = pe.matmul(wide("t", b, g)[:, n * (S - q0):(n + 1) * (S - q0)], k[0:HM, h, kt * P:(kt + 1) * P],
                                   q[0:HM, h, q0:S], start=True, stop=True)
                mm.then_inc(full["t"], 1)

            def attend(b):
                pe.wait_ge(v_copied, b + 1)
                pe.wait_ge(masked, SG * (b + 1))
                v = vs[b % 3]
                for t in range(QT):
                    take("o", b, t)
                    for h in range(NH):
                        dst = narrow("o", b, t)[:, h * (HD + 1):(h + 1) * (HD + 1)]
                        p0 = probs[:, h // 4, (h % 4) * S + t * P:(h % 4) * S + (t + 1) * P]
                        mm = pe.matmul(dst, p0, v[:, 0, h], start=True, stop=(t == 0))
                        if t == 1:
                            p1 = probs[:, 4 + h // 8, (h % 8) * P:(h % 8 + 1) * P]
                            mm = pe.matmul(dst, p1, v[:, 1, h], start=False, stop=True)
                    mm.then_inc(full["o"], 1)

            def turn(kind, n, tiles):
                take(kind, n)
                for k in range(KD):
                    for t in range(2):
                        mm = pe.transpose(narrow(kind, n)[:, k * S + t * P:k * S + (t + 1) * P],
                                          tiles[t][:, k * P:(k + 1) * P], ident[:])
                mm.then_inc(full[kind], 1)

            def by_weights(kind, n, xh, xl, col):
                take(kind, n)
                for t in range(2):
                    for k in range(KD):
                        c = col + k * D
                        mm = three(narrow(kind, n)[:, t * D:(t + 1) * D], xh[:, k, t * P:(t + 1) * P],
                                   xl[:, k, t * P:(t + 1) * P], w_h[:, c:c + D], w_l[:, c:c + D], k == 0, k == KD - 1)
                mm.then_inc(full[kind], 1)

            def tail(b, g):
                if g == 0:
                    pe.wait_ge(attn_done, 2 * b + 2)
                    if b == 0:
                        pe.wait_ge(pool_const, 6)
                    turn("at", b, [attn[:, t] for t in range(QT)])
                if g == 1:
                    pe.wait_ge(hi["at"], b + 1)
                    pe.wait_ge(lo["at"], b + 1)
                    if b == 0:
                        pe.wait_ge(wr_l, 5)
                    by_weights("wo", b, aT_h, aT_l, W_O)
                if g == 3:
                    pe.wait_ge(normed, 2 * b + 2)
                    turn("xt", b, [resid[:, b, t] for t in range(QT)])
                if g == 4:
                    pe.wait_ge(hi["xt"], b + 1)
                    pe.wait_ge(lo["xt"], b + 1)
                    by_weights("gate", b, x1T_h, x1T_l, W_G)
                    take("xq", b)
                    for h in range(XH):
                        c = W_H + h * P
                        mm = three(narrow("xq", b)[:, h * S:(h + 1) * S], w_h[:, c:c + P], w_l[:, c:c + P],
                                   x1T_h[:, h], x1T_l[:, h], True, True)
                    mm.then_inc(full["xq"], 1)

            for b in range(2):
                project_qk(b)
                project_v(b)
            for g in range(SG):
                scores(0, g)
            max_rows(0)
            for i in range(B):
                if i + 2 < B:
                    project_qk(i + 2)
                    project_v(i + 2)
                for g in range(SG):
                    if i + 1 < B:
                        scores(i + 1, g)
                    scores_T(i, g)
                    if i >= 1:
                        tail(i - 1, g)
                attend(i)
                if i + 1 < B:
                    max_rows(i + 1)

            pe.wait_ge(cT_lo, 2)
            pe.wait_ge(cT_hi, 2)
            for c in range(2):
                take("xk", c)
                for h in range(XH):
                    w0 = W_H + h * P
                    mm = three(wide("xk", c)[:, h * 512:(h + 1) * 512], w_h[:, w0:w0 + P], w_l[:, w0:w0 + P],
                               cT_h[:, h, c * 512:(c + 1) * 512], cT_l[:, h, c * 512:(c + 1) * 512], True, True)
                mm.then_inc(full["xk"], 1)

            def values(c):
                take("xv", c)
                for n in range(4):
                    s0 = c * 512 + n * P
                    for h in range(XH):
                        w0 = W_H + h * P
                        mm = three(wide("xv", c)[:, n * 256 + h * P:n * 256 + (h + 1) * P], cT_h[:, h, s0:s0 + P],
                                   cT_l[:, h, s0:s0 + P], w_h[:, w0:w0 + P], w_l[:, w0:w0 + P], True, True)
                mm.then_inc(full["xv"], 1)

            tail(B - 1, 0)
            values(0)
            tail(B - 1, 1)
            values(1)
            tail(B - 1, 3)
            tail(B - 1, 4)
            pe.wait_ge(hi["xk"], 2)
            pe.wait_ge(lo["xk"], 2)
            pe.wait_ge(hi["xq"], B)
            pe.wait_ge(lo["xq"], B)
            for h in range(XH):
                take("sx", h)
                for t in range(QT):
                    q0, c0 = t * P, t * S
                    for b in range(B):
                        k0 = b * S + t * P
                        mm = three(narrow("sx", h)[:, c0:c0 + S - q0], xk_h[:, h, k0:k0 + P], xk_l[:, h, k0:k0 + P],
                                   xq_h[:, h, b, q0:S], xq_l[:, h, b, q0:S], b == 0, b == B - 1)
                mm.then_inc(full["sx"], 1)
            pe.wait_ge(hi["xv"], B)
            pe.wait_ge(lo["xv"], B)
            pe.wait_ge(ones_ready, 7)
            for t in range(QT):
                take("ox", t)
                for h in range(XH):
                    pe.wait_ge(rA_lo, h + 1)
                    dst = wide("ox", t)[:, h * 512:(h + 1) * 512]
                    v0h, v0l, v1h, v1l = (v[:, k, h].rearrange("p b e -> p (b e)") for k in range(QT) for v in (xv_h, xv_l))
                    three(dst, rA_h[:, h, t * P:(t + 1) * P], rA_l[:, h, t * P:(t + 1) * P], v0h, v0l, True, False)
                    if t == 0:
                        pe.matmul(dst, ones_r[:], v1h, start=False, stop=False)
                        mm = pe.matmul(dst, ones_r[:], v1l, start=False, stop=True)
                    else:
                        mm = three(dst, rA_h[:, h, 256:384], rA_l[:, h, 256:384], v1h, v1l, False, True)
                mm.then_inc(full["ox"], 1)

            def y_turn(q):
                t, b0 = q // 2, 2 * (q % 2)
                pe.wait_ge(y_done, B * t + b0 + 2)
                turn("yt", q, [y[:, t, b0 + j] for j in range(2)])

            def second(q):
                pe.wait_ge(hi["yt"], q + 1)
                pe.wait_ge(lo["yt"], q + 1)
                by_weights("w2", q, yT_h, yT_l, W_O2)

            def x2_turn(q):
                t, b0 = q // 2, 2 * (q % 2)
                pe.wait_ge(normed, 2 * B + 2 * q + 2)
                turn("x2t", q, [resid[:, b0 + j, t] for j in range(2)])

            def vectors(u):
                q, j = u // 2, u % 2
                take("ve", u)
                pe.wait_ge(hi["x2t"], q + 1)
                pe.wait_ge(lo["x2t"], q + 1)
                if u == 0:
                    pe.wait_ge(ea_lo, KD)
                for c in range(2):
                    for k in range(KD):
                        mm = three(wide("ve", u)[:, c * 512:(c + 1) * 512], x2T_h[:, q, k, j * P:(j + 1) * P],
                                   x2T_l[:, q, k, j * P:(j + 1) * P], ea_h[:, k, c * 512:(c + 1) * 512],
                                   ea_l[:, k, c * 512:(c + 1) * 512], k == 0, k == KD - 1)
                mm.then_inc(full["ve"], 1)

            def z_turn(u):
                take("zt", u)
                pe.wait_ge(z_done, u + 1)
                for k in range(ER // P):
                    mm = pe.transpose(wide("zt", u)[:, k * P:(k + 1) * P], z[u % 2][:, k * P:(k + 1) * P], ident[:])
                mm.then_inc(full["zt"], 1)

            def experts(u):
                q, j = u // 2, u % 2
                take("d", u)
                dst = narrow("d", u)[:, 0:D]
                for k in range(KD):
                    c = W_F + k * D
                    three(dst, x2T_h[:, q, k, j * P:(j + 1) * P], x2T_l[:, q, k, j * P:(j + 1) * P],
                          w_h[:, c:c + D], w_l[:, c:c + D], k == 0, False)
                pe.wait_ge(hi["zt"], u + 1)
                pe.wait_ge(lo["zt"], u + 1)
                if u == 0:
                    pe.wait_ge(eb_lo, 2)
                for k in range(ER // P):
                    mm = three(dst, zT_h[:, k], zT_l[:, k], eb_h[:, k], eb_l[:, k], False, k == ER // P - 1)
                mm.then_inc(full["d"], 1)

            y_turn(0)
            second(0)
            y_turn(1)
            second(1)
            y_turn(2)
            x2_turn(0)
            second(2)
            y_turn(3)
            vectors(0)
            second(3)
            x2_turn(1)
            vectors(1)
            x2_turn(2)
            x2_turn(3)
            for u in range(2, FFN_TILES + 3):
                if u < FFN_TILES:
                    vectors(u)
                if 0 <= u - 3 < FFN_TILES:
                    experts(u - 3)
                if 0 <= u - 2 < FFN_TILES:
                    z_turn(u - 2)


def _decay():
    import numpy as np
    idx = np.arange(S, dtype=np.float32)
    out = np.zeros((P, XH, 384), np.float32)
    for h in range(XH):
        gam = np.float64(1.0 - 2.0 ** (-5.0 - h))
        expo = idx[None, :] - idx[:, None]
        d = np.where(expo <= 0, gam ** np.minimum(expo, 0), 0.0)
        d = (d / np.sqrt(d.sum(-1))[None, :] / np.sqrt(128.0)).T.astype(np.float32)
        out[:, h, 0:S] = d[0:P]
        out[:, h, S:] = d[P:, P:]
    return out


def kernel(x, ctx_2048, L0_attn_w_qkv, L0_attn_w_o, L0_xattn_Wh, L0_xattn_wg_w, L0_xattn_wo_w, L0_xattn_gn_gamma,
           L0_xattn_gn_beta, L0_ffn_A, L0_ffn_B, L0_ffn_W, L0_ffn_bias):
    import numpy as np
    import concourse.bacc as bacc
    from concourse.bass_utils import run_bass_kernel_spmd

    def rows(a):
        a = np.asarray(a)
        return a.reshape(a.shape[0] // P, P, a.shape[1]).transpose(1, 0, 2)

    def flat(a):
        return a.reshape(P, -1)

    def heads(a):
        return np.asarray(a).reshape(HB, 2, HD, D).transpose(1, 2, 0, 3).reshape(D, D)

    wqkv = np.asarray(L0_attn_w_qkv)
    wqk = np.concatenate([heads(wqkv[0:D]), heads(wqkv[D:2 * D])], 0)
    w = np.concatenate([flat(rows(wqk.T)), flat(rows(wqkv[2 * D:].T)), flat(rows(np.asarray(L0_attn_w_o).T)),
                        flat(np.asarray(L0_xattn_Wh).transpose(1, 0, 2)), flat(rows(L0_xattn_wg_w)),
                        flat(rows(L0_xattn_wo_w)), flat(rows(np.asarray(L0_ffn_W).T))], 1)
    a = np.asarray(L0_ffn_A).reshape(ER, D).T
    b = np.asarray(L0_ffn_B).transpose(0, 2, 1).reshape(ER, D)
    xf, cf = np.asarray(x).reshape(B * S, D), np.asarray(ctx_2048).reshape(B * S, D)
    arrays = {
        "x": np.asarray(x).reshape(B, QT, P, D).transpose(2, 0, 1, 3),
        "xT": rows(xf.T), "cT": rows(cf.T), "w": w, "aT": flat(rows(a)), "bT": flat(rows(b)),
        "gam": np.broadcast_to(np.asarray(L0_xattn_gn_gamma), (P, D)),
        "bet": np.broadcast_to(np.asarray(L0_xattn_gn_beta), (P, D)),
        "bias": np.broadcast_to(np.asarray(L0_ffn_bias), (P, D)),
        "decay": _decay(),
    }
    arrays = {k + "_dram": np.ascontiguousarray(v) for k, v in arrays.items()}
    nc = bacc.Bacc("TRN2", target_bir_lowering=False, num_devices=1)
    args = [nc.dram_tensor(k, v.shape, mybir.dt.from_np(v.dtype), kind="ExternalInput").ap() for k, v in arrays.items()]
    args.append(nc.dram_tensor("out_dram", (P, B, QT, D), F32, kind="ExternalOutput").ap())
    decoder_layer(nc, *args)
    r = run_bass_kernel_spmd(nc, [arrays], core_ids=[0])
    got = r.results[0]["out_dram"]
    return np.ascontiguousarray(got.transpose(1, 2, 0, 3).reshape(B, S, D))
```

```python
from contextlib import ExitStack

import concourse.bass as bass
from concourse import mybir

F32 = mybir.dt.float32
F32R = mybir.dt.float32r
BF16 = mybir.dt.bfloat16
U32 = mybir.dt.uint32
ALU = mybir.AluOpType
ACT = mybir.ActivationFunctionType
AX = mybir.AxisListType

P = 128
B, S, D = 4, 256, 256
KD = D // P
QT = S // P
NH, HD = 16, 16
XH = 2
EXP, RANK, TOPK = 64, 16, 4
ER = EXP * RANK
NEG = -3.0e38
HI = 3 * HD
HM = HI + 2
HB = 8
SG = 6

W_QK, W_V, W_O, W_H, W_G, W_O2, W_F = 0, 1024, 1536, 2048, 2304, 2816, 3328
W_N = 3840
W_CHUNKS = ((W_QK, W_V), (W_V, W_O), (W_O, W_N))
VW = 32
FFN_TILES = B * QT


def ffn_tile(u):
    q = u // 2
    return 2 * (q % 2) + u % 2, q // 2


def schedule():
    def norm(kind, n):
        return [(kind, n), ("pow", kind, n), ("norm", kind, n)]

    steps = [("xs", 0), ("qk", 0), ("xs", 1), ("v", 0), ("wr",), ("qk", 1), ("v", 1)]
    for g in range(SG):
        steps.append(("s", 0, g))
        if g == 2:
            steps.append(("xs", 2))
    steps += [("nm", 0), ("mt", 0)]
    for i in range(B):
        if i + 2 < B:
            steps.append(("qk", i + 2))
        if i >= 1:
            steps.append(("o", i - 1))
        for g in range(SG):
            if i + 1 < B:
                steps.append(("s", i + 1, g))
            steps.append(("t", i, g))
            if i >= 1 and g == 1:
                steps.append(("at", i - 1))
            if i >= 1 and g == 2:
                steps += [("wo", i - 1)] + norm("n1", i - 1)
            if g == 3 and i + 3 < B:
                steps.append(("xs", i + 3))
            if i >= 1 and g == 4:
                steps.append(("xt", i - 1))
        if i + 1 < B:
            steps.append(("nm", i + 1))
        if i >= 1:
            steps += [("gate", i - 1), ("xq", i - 1)]
        if i + 2 < B:
            steps.append(("v", i + 2))
        steps.append(("ot", i))
        if i + 1 < B:
            steps.append(("mt", i + 1))
    L = B - 1
    steps += [("o", L), ("cs", 0), ("cs", 1), ("at", L), ("xk", 0), ("wo", L)] + norm("n1", L)
    steps += [("xk", 1), ("xv", 0), ("xv", 1), ("xt", L), ("gate", L), ("xq", L), ("ab", 0), ("ab", 1), ("sx", 0),
              ("sx", 1), ("ra", 0), ("ra", 1), ("ab", 2), ("ab", 3),
              ("ox", 0), ("gs", 0), ("pow", "gs", 0), ("ox", 1), ("gs", 1), ("pow", "gs", 1), ("ga", 0, 0), ("ga", 0, 1),
              ("yt", 0), ("ga", 0, 2), ("ga", 0, 3), ("w2", 0), ("yt", 1)] + norm("n2", 0)
    steps += [("ga", 1, 0), ("ga", 1, 1), ("w2", 1), ("x2t", 0)] + norm("n2", 1)
    steps += [("yt", 2), ("ga", 1, 2), ("ga", 1, 3), ("ve", 0), ("w2", 2), ("x2t", 1), ("route", 0)] + norm("n2", 2)
    steps += [("pick", 0), ("yt", 3), ("ve", 1), ("sum", 0), ("spread", 0), ("w2", 3), ("x2t", 2), ("route", 1)]
    steps += norm("n2", 3) + [("pick", 1)]
    for u in range(2, FFN_TILES + 2):
        steps.append(("zt", u - 2))
        if u >= 3:
            steps.append(("norm", "n3", u - 3))
        if u < FFN_TILES:
            steps.append(("ve", u))
        if u == 2:
            steps.append(("x2t", 3))
        if u - 1 < FFN_TILES:
            steps += [("sum", u - 1), ("spread", u - 1)]
        if u < FFN_TILES:
            steps += [("route", u), ("pick", u)]
        steps += [("d", u - 2), ("n3", u - 2), ("pow", "n3", u - 2)]
    steps.append(("norm", "n3", FFN_TILES - 1))
    return steps


STEPS = schedule()
WIDE_SLOTS, NARROW_SLOTS = 3, 2
WIDE = [k for k in STEPS if k[0] in ("qk", "s", "t", "ot", "xk", "xv", "ox", "ve", "zt")]
NARROW = [k for step in STEPS for k in ([("o", step[1], t) for t in range(QT)] if step[0] == "o" else [step])
          if k[0] in ("v", "mt", "o", "at", "wo", "xt", "gate", "xq", "sx", "yt", "w2", "x2t", "d")]
SLOT = {k: n % WIDE_SLOTS for n, k in enumerate(WIDE)}
SLOT.update({k: n % NARROW_SLOTS for n, k in enumerate(NARROW)})
BEFORE = {k: WIDE[n - WIDE_SLOTS] for n, k in enumerate(WIDE) if n >= WIDE_SLOTS}
BEFORE.update({k: NARROW[n - NARROW_SLOTS] for n, k in enumerate(NARROW) if n >= NARROW_SLOTS})
NORMS = [k for k in STEPS if k[0] in ("n1", "gs", "n2", "n3")]
NORM_NO = {k: n for n, k in enumerate(NORMS)}
SETS = 3
SUMS = [k for k in NORMS if k[0] != "gs"]
SUM_NO = {k: n for n, k in enumerate(SUMS)}


def decoder_layer(nc, x, xT, cT, w, aT, bT, gam, bet, bias, decay, out):
    with ExitStack() as ctx:
        def sb(name, shape, dt=F32, stack=ctx):
            return stack.enter_context(nc.sbuf_tensor(name, shape, dt))

        def sem(name):
            return ctx.enter_context(nc.semaphore(name))

        ident = sb("ident", [P, P])
        ident_bf = sb("ident_bf", [P, P], BF16)
        causal = sb("causal", [P, 2 * P], BF16)
        iota = sb("iota", [P, EXP])
        neg_half = sb("neg_half", [P, 4])
        w_raw = sb("w_raw", [P, 4096])
        w_h = sb("w_h", [P, W_N], F32R)
        w_l = sb("w_l", [P, W_N], F32R)
        resid = sb("resid", [P, B, QT, D])
        act_raw = sb("act_raw", [P, KD, B * S])
        x1T_h = sb("x1T_h", [P, KD, S], F32R)
        x1T_l = sb("x1T_l", [P, KD, S], F32R)
        xq_h = sb("xq_h", [P, XH, B, S], F32R)
        xq_l = sb("xq_l", [P, XH, B, S], F32R)
        gb = sb("gb", [P, B, QT, D])
        gg = sb("gg", [P, B, QT, D])
        gam_b = sb("gam_b", [P, D])
        bet_b = sb("bet_b", [P, D])
        bias_b = sb("bias_b", [P, D])
        pre = [sb(f"pre{i}", [P, 2, D]) for i in range(2)]
        stats = [sb(f"stats{i}", [P, 4, 6]) for i in range(SETS)]
        mv = [sb(f"mv{i}", [P, 4, 2]) for i in range(SETS)]
        var_eps = [sb(f"var_eps{i}", [P, 4]) for i in range(SETS)]
        neg_mean = [sb(f"neg_mean{i}", [P, 4]) for i in range(SETS)]
        rstd = [sb(f"rstd{i}", [P, 4]) for i in range(SETS)]
        shift = [sb(f"shift{i}", [P, 4]) for i in range(SETS)]
        rden = sb("rden", [P, QT, NH])
        attn = sb("attn", [P, QT, D])
        aT_h = sb("aT_h", [P, KD, S], F32R)
        aT_l = sb("aT_l", [P, KD, S], F32R)
        att = ExitStack()
        xT_h = [sb(f"xT_h{i}", [P, KD, S], F32R, att) for i in range(2)]
        xT_l = [sb(f"xT_l{i}", [P, KD, S], F32R, att) for i in range(2)]
        qk_h = sb("qk_h", [P, 4, S], F32R, att)
        qk_l = sb("qk_l", [P, 4, S], F32R, att)
        q_st = sb("q_st", [P, NH, S], F32R, att)
        k_st = sb("k_st", [P, NH, S], F32R, att)
        vs = [sb(f"vs{i}", [P, QT, NH, VW], F32, att) for i in range(2)]
        probs = sb("probs", [P, SG, 1024], F32, att)
        nm = sb("nm", [P, QT, NH], F32, att)
        nm_hl = sb("nm_hl", [P, QT, 2, NH], F32R, att)
        nmT = sb("nmT", [2 * NH, S], F32R, att)
        oT = sb("oT", [P, 4, S], F32, att)
        att.close()
        ea_h = sb("ea_h", [P, KD, ER], F32R)
        ea_l = sb("ea_l", [P, KD, ER], F32R)
        eb_h = sb("eb_h", [P, ER // P, D], F32R)
        eb_l = sb("eb_l", [P, ER // P, D], F32R)
        yT_h, yT_l = aT_h, aT_l
        ret = ExitStack()
        cT_h = sb("cT_h", [P, KD, B * S], F32R, ret)
        cT_l = sb("cT_l", [P, KD, B * S], F32R, ret)
        xk_h = sb("xk_h", [P, XH, B * S], F32R, ret)
        xk_l = sb("xk_l", [P, XH, B * S], F32R, ret)
        xv_h = sb("xv_h", [P, QT, XH, B, P], F32R, ret)
        xv_l = sb("xv_l", [P, QT, XH, B, P], F32R, ret)
        dec = sb("dec", [P, XH, 384], F32, ret)
        mag = sb("mag", [P, XH, 384], F32, ret)
        rA_h = sb("rA_h", [P, XH, 384], F32R, ret)
        rA_l = sb("rA_l", [P, XH, 384], F32R, ret)
        ones_r = sb("ones_r", [P, P], F32R, ret)
        ret.close()
        x2T_h = sb("x2T_h", [P, 4, KD, S], F32R)
        x2T_l = sb("x2T_l", [P, 4, KD, S], F32R)
        sq = sb("sq", [P, ER])
        vc = [sb(f"vc{i}", [P, ER]) for i in range(2)]
        n2 = sb("n2", [P, EXP])
        top = sb("top", [P, 8])
        idx = sb("idx", [P, 8], U32)
        eq = sb("eq", [P, EXP, TOPK])
        route = [sb(f"route{i}", [P, EXP]) for i in range(2)]
        vr = [sb(f"vr{i}", [P, RANK]) for i in range(2)]
        z = [sb(f"z{i}", [P, ER]) for i in range(2)]
        zT_h = sb("zT_h", [P, ER // P, P], F32R)
        zT_l = sb("zT_l", [P, ER // P, P], F32R)
        res = [sb(f"res{i}", [P, D]) for i in range(2)]

        wide_ps = [ctx.enter_context(nc.psum_tensor(f"wide{i}", [P, 1024], F32)) for i in range(WIDE_SLOTS)]
        narrow_ps = [ctx.enter_context(nc.psum_tensor(f"narrow{i}", [P, 512], F32)) for i in range(NARROW_SLOTS)]

        def wide(*key):
            return wide_ps[SLOT[key]]

        def narrow(*key):
            return narrow_ps[SLOT[key]]

        def flat(v):
            return v.rearrange("p k s -> p (k s)")

        ld_x = [sem(f"ld_x{b}") for b in range(B)]
        ld_w = [sem(f"ld_w{n}") for n in range(3)]
        ld_c, ld_res, ld_a, ld_b, ld_dec = (sem(n) for n in ("ld_c", "ld_res", "ld_a", "ld_b", "ld_dec"))
        ld_vec = [sem(f"ld_vec{n}") for n in range(3)]
        stacked = [sem(f"stacked{i}") for i in range(2)]
        nm_stacked = [sem(f"nm_stacked{i}") for i in range(2)]
        stored = [sem(f"stored{i}") for i in range(2)]
        pool_const, iota_ready, ones_ready, v_ones, ones_r_ready = (
            sem(n) for n in ("pool_const", "iota_ready", "ones_ready", "v_ones", "ones_r_ready"))
        w_hi = [sem(f"w_hi{n}") for n in range(3)]
        w_lo = [sem(f"w_lo{n}") for n in range(3)]
        xT_hi, xT_lo, cT_hi, cT_lo, ab_hi, ab_lo = (sem(n) for n in ("xT_hi", "xT_lo", "cT_hi", "cT_lo", "ab_hi", "ab_lo"))
        full = {k: sem("pe_" + k) for k in ("qk", "v", "s", "mt", "t", "ot", "o", "at", "wo", "xt", "gate", "xq", "xk",
                                            "xv", "sx", "ox", "yt", "w2", "x2t", "ve", "zt", "d")}
        hi = {k: sem(k + "_hi") for k in ("qk", "at", "xt", "xq", "xk", "xv", "yt", "x2t", "zt")}
        lo = {k: sem(k + "_lo") for k in ("qk", "at", "xt", "xq", "xk", "xv", "yt", "x2t", "zt")}
        v_copied, maxed, nm_hi, nm_lo, nmT_copied, exped, cut_done, oT_copied, rden_done, attn_done = (
            sem(n) for n in ("v_copied", "maxed", "nm_hi", "nm_lo", "nmT_copied", "exped", "cut_done", "oT_copied",
                             "rden_done", "attn_done"))
        gated, gg_done, gb_done = (sem(n) for n in ("gated", "gg_done", "gb_done"))
        added, stat_done, mv_done, var_done, neg_done, rstd_done, shift_done = (sem(n) for n in (
            "added", "stat_done", "mv_done", "var_done", "neg_done", "rstd_done", "shift_done"))
        normed = {k: sem("normed_" + k) for k in ("n1", "gs", "n2", "n3")}
        abs_done, decayed, rA_hi, rA_lo, y_mul, y_done = (sem(n) for n in (
            "abs_done", "decayed", "rA_hi", "rA_lo", "y_mul", "y_done"))
        squared, vc_done, n2_done, top_done, idx_done, eq_done, routed = (sem(n) for n in (
            "squared", "vc_done", "n2_done", "top_done", "idx_done", "eq_done", "routed"))
        picked, v_done, z_done, biased = (sem(n) for n in ("picked", "v_done", "z_done", "biased"))

        def released(key):
            k, n = key[0], key[1:]
            if k in ("qk", "at", "xt", "xq", "xk", "yt", "x2t", "zt"):
                return lo[k], n[0] + 1
            if k in ("wo", "w2", "d"):
                return added, SUM_NO[{"wo": "n1", "w2": "n2", "d": "n3"}[k], n[0]] + 1
            return {
                "xv": lambda: (lo["xv"], 2 * n[0] + 2),
                "v": lambda: (v_copied, n[0] + 1),
                "s": lambda: (maxed, SG * n[0] + n[1] + 1),
                "mt": lambda: (nmT_copied, n[0] + 1),
                "t": lambda: (exped, SG * n[0] + n[1] + 1),
                "ot": lambda: (oT_copied, n[0] + 1),
                "o": lambda: (attn_done, QT * n[0] + n[1] + 1),
                "gate": lambda: (gated, n[0] + 1),
                "sx": lambda: (abs_done, n[0] + 1),
                "ox": lambda: (normed["gs"], B * n[0] + B),
                "ve": lambda: (vc_done, n[0] + 1),
            }[k]()

        def norm_tiles(key):
            return {"n1": 2, "gs": 4, "n2": 2, "n3": 1}[key[0]]

        def over(old):
            return normed[old[0]], norm_tiles(old) * (old[1] + 1)

        block = ctx.enter_context(nc.Block())

        @block.sync
        def _(sp):
            sp.dma_start(act_raw[:, :, 0:S], xT[:, :, 0:S]).then_inc(ld_x[0], 16)
            for b in range(1, B):
                sp.dma_start(act_raw[:, :, b * S:(b + 1) * S], xT[:, :, b * S:(b + 1) * S]).then_inc(ld_x[b], 16)
            for n, (dst, src) in enumerate(((gam_b, gam), (bet_b, bet), (bias_b, bias))):
                sp.dma_start(dst[:], src).then_inc(ld_vec[n], 16)
            sp.dma_start(resid[:], x).then_inc(ld_res, 16)

            def stack_scores(b):
                sp.wait_ge(hi["qk"], b + 1)
                sp.wait_ge(lo["qk"], b + 1)
                if b < 2:
                    sp.wait_ge(ones_ready, 2)
                else:
                    sp.wait_ge(full["t"], SG * (b - 1))
                for n, (q, k) in enumerate(((qk_h, qk_h), (qk_h, qk_l), (qk_l, qk_h))):
                    rows = slice(64 * (b % 2) + HD * n, 64 * (b % 2) + HD * (n + 1))
                    sp.dma_start(q_st[rows].bitcast(F32), q[:, 0:2, :].bitcast(F32)).then_inc(stacked[b % 2], 16)
                    sp.dma_start(k_st[rows].bitcast(F32), k[:, 2:4, :].bitcast(F32)).then_inc(stacked[b % 2], 16)

            def stack_max(b):
                sp.wait_ge(nmT_copied, b + 1)
                if b >= 2:
                    sp.wait_ge(full["t"], SG * (b - 1))
                row = 64 * (b % 2) + HI
                sp.dma_start(q_st[row:row + 2].bitcast(F32), nmT[:].bitcast(F32)).then_inc(nm_stacked[b % 2], 16)

            def after_wr():
                sp.wait_ge(w_lo[2], 1)
                sp.wait_ge(w_lo[1], 1)
                sp.wait_ge(w_lo[0], 1)
                sp.dma_start(w_raw[:, 0:2048], aT).then_inc(ld_a, 16)
                sp.dma_start(w_raw[:, 2048:4096], bT).then_inc(ld_b, 16)

            def after_split_x():
                sp.wait_ge(xT_lo, B)
                sp.dma_start(act_raw[:], cT).then_inc(ld_c, 16)

            def load_decay():
                sp.wait_ge(full["o"], 2 * B)
                sp.dma_start(dec[:], decay).then_inc(ld_dec, 16)

            def store(u):
                b, t = ffn_tile(u)
                sp.wait_ge(normed["n3"], u + 1)
                sp.dma_start(out[:, b, t, :], res[u % 2][:]).then_inc(stored[u % 2], 16)

            for step in STEPS:
                k, n = step[0], step[1:]
                if k == "qk":
                    stack_scores(*n)
                    if n[0] == 1:
                        after_wr()
                    if n[0] == B - 1:
                        after_split_x()
                elif k == "mt":
                    stack_max(*n)
                elif step == ("cs", 0):
                    load_decay()
                elif k == "norm" and n[0] == "n3":
                    store(n[1])
            for i in range(2):
                sp.wait_ge(stored[i], 16 * (FFN_TILES // 2))

        @block.scalar
        def _(act):
            for n, (a, b) in enumerate(W_CHUNKS):
                act.dma_start(w_raw[:, a:b], w[:, a:b]).then_inc(ld_w[n], 16)

            def w_split(n):
                a, b = W_CHUNKS[n]
                act.wait_ge(ld_w[n], 16)
                act.activation(w_h[:, a:b], w_raw[:, a:b], ACT.Copy).then_inc(w_hi[n], 1)

            def split_x(b):
                act.wait_ge(ld_x[b], 16)
                if b >= 2:
                    act.wait_ge(full["qk"], b - 1)
                    act.wait_ge(full["v"], b - 1)
                act.activation(xT_h[b % 2][:], act_raw[:, :, b * S:(b + 1) * S], ACT.Copy).then_inc(xT_hi, 1)
                if b < 2:
                    w_split(b)

            def split_hi(kind, n, dst, src):
                act.wait_ge(full[kind], n + 1)
                act.activation(dst, src, ACT.Copy).then_inc(hi[kind], 1)

            def qk(b):
                if b >= 1:
                    act.wait_ge(stacked[(b - 1) % 2], 96 * ((b - 1) // 2 + 1))
                split_hi("qk", b, qk_h[:], wide("qk", b)[:].rearrange("p (m s) -> p m s", m=4))

            def v(b):
                act.wait_ge(full["v"], b + 1)
                if b < 2:
                    act.wait_ge(v_ones, b + 1)
                else:
                    act.wait_ge(full["ot"], b - 1)
                act.activation(vs[b % 2][:].rearrange("p t h e -> p (t h) e")[:, :, 0:HD],
                               narrow("v", b)[:].rearrange("p (n d) -> p n d", d=HD), ACT.Copy)\
                   .then_inc(v_copied, 1)

            def mt(b):
                act.wait_ge(full["mt"], b + 1)
                if b >= 1:
                    act.wait_ge(nm_stacked[(b - 1) % 2], 16 * ((b - 1) // 2 + 1))
                act.activation(nmT[:], narrow("mt", b)[0:2 * NH, 0:S], ACT.Copy).then_inc(nmT_copied, 1)

            def t(b, g):
                act.wait_ge(full["t"], SG * b + g + 1)
                if b >= 1:
                    act.wait_ge(full["ot"], b)
                act.activation(probs[:, g, :], wide("t", b, g)[:], ACT.Exp, scale=HD ** -0.5).then_inc(exped, 1)

            def ot(b):
                act.wait_ge(full["ot"], b + 1)
                if b >= 1:
                    act.wait_ge(full["o"], 2 * b)
                act.activation(flat(oT[:]), wide("ot", b)[:], ACT.Copy).then_inc(oT_copied, 1)

            def at(b):
                if b >= 1:
                    act.wait_ge(full["wo"], b)
                split_hi("at", b, flat(aT_h[:]), narrow("at", b)[:])

            def xt(b):
                if b >= 1:
                    act.wait_ge(full["xq"], b)
                split_hi("xt", b, flat(x1T_h[:]), narrow("xt", b)[:])

            def gate(b):
                act.wait_ge(full["gate"], b + 1)
                act.activation(flat(gb[:, b]), narrow("gate", b)[:], ACT.Relu).then_inc(gated, 1)

            def xq(b):
                split_hi("xq", b, xq_h[:, :, b, :], narrow("xq", b)[:].rearrange("p (h s) -> p h s", h=XH))

            def split_context(c):
                if c == 0:
                    act.wait_ge(ld_c, 16)
                    act.wait_ge(full["o"], 2 * B)
                    act.activation(ones_r[:], ident[:], ACT.Copy, scale=0.0, bias=1.0).then_inc(ones_r_ready, 1)
                v_ = slice(c * 512, c * 512 + 512)
                act.activation(cT_h[:, :, v_], act_raw[:, :, v_], ACT.Copy).then_inc(cT_hi, 1)

            def xk(c):
                split_hi("xk", c, xk_h[:, :, c * 512:c * 512 + 512], wide("xk", c)[:].rearrange("p (h s) -> p h s", h=XH))

            def xv(c):
                act.wait_ge(full["xv"], c + 1)
                for n in range(2):
                    act.activation(xv_h[:, :, :, 2 * c + n, :],
                                   wide("xv", c)[:, n * 512:n * 512 + 512].rearrange("p (t h e) -> p t h e", t=QT, h=XH),
                                   ACT.Copy).then_inc(hi["xv"], 1)

            def experts_hi(n):
                act.wait_ge((ld_a, ld_b)[n // 2], 16)
                dst = ea_h[:, n] if n < 2 else flat(eb_h[:, 4 * n - 8:4 * n - 4])
                act.activation(dst, w_raw[:, n * 1024:(n + 1) * 1024], ACT.Copy).then_inc(ab_hi, 1)

            def sx(h):
                act.wait_ge(full["sx"], h + 1)
                act.activation(mag[:, h], narrow("sx", h)[:, 0:384], ACT.Abs).then_inc(abs_done, 1)

            def normalise(key, j, dst, src):
                i = NORM_NO[key] % SETS
                act.wait_ge(shift_done, NORM_NO[key] + 1)
                act.activation(dst, src, ACT.Identity, bias=shift[i][:, j:j + 1], scale=rstd[i][:, j:j + 1])\
                   .then_inc(normed[key[0]], 1)

            def norm(kind, n):
                for j in range(norm_tiles((kind, n))):
                    src = pre[SUM_NO[kind, n] % 2][:, j]
                    if kind == "n1":
                        dst = resid[:, n, j]
                    elif kind == "n2":
                        b, tt = ffn_tile(2 * n + j)
                        dst = resid[:, b, tt]
                    else:
                        if n >= 2:
                            act.wait_ge(stored[n % 2], 16 * (n // 2))
                        dst = res[n % 2][:]
                    normalise((kind, n), j, dst, src)

            def ga(tt, b):
                if B * tt + b >= 2:
                    act.wait_ge(y_mul, B * tt + b - 1)
                o = wide("ox", tt)[:].rearrange("p (h b e) -> p b h e", h=XH, b=B)[:, b]
                normalise(("gs", tt), b, attn[:, b % 2].rearrange("p (h e) -> p h e", h=XH), o)

            def yt(q):
                if q >= 1:
                    act.wait_ge(full["w2"], q)
                split_hi("yt", q, flat(yT_h[:]), narrow("yt", q)[:])

            def x2t(q):
                act.wait_ge(full["ox"], 2)
                split_hi("x2t", q, flat(x2T_h[:, q]), narrow("x2t", q)[:])

            def ve(u):
                act.wait_ge(full["ve"], u + 1)
                act.wait_ge(y_done, 2 * B)
                if u >= 1:
                    act.wait_ge(n2_done, u)
                act.activation(sq[:], wide("ve", u)[:], ACT.Square).then_inc(squared, 1)
                if u >= 2:
                    act.wait_ge(v_done, u - 1)
                act.activation(vc[u % 2][:], wide("ve", u)[:], ACT.Copy, scale=1.0 / TOPK ** 2).then_inc(vc_done, 1)

            def zt(u):
                if u >= 1:
                    act.wait_ge(full["d"], u)
                split_hi("zt", u, flat(zT_h[:]), wide("zt", u)[:])

            parts = {"xs": split_x, "wr": lambda: w_split(2), "qk": qk, "v": v, "mt": mt, "t": t, "ot": ot, "at": at,
                     "norm": norm, "xt": xt, "gate": gate, "xq": xq, "cs": split_context, "xk": xk, "xv": xv,
                     "ab": experts_hi, "sx": sx, "ga": ga, "yt": yt, "x2t": x2t, "ve": ve, "zt": zt}
            for step in STEPS:
                if step[0] in parts:
                    parts[step[0]](*step[1:])

        @block.gpsimd
        def _(pool):
            pool.memset(ident[:], 0.0).then_inc(pool_const, 1)
            pool.memset(causal[:], 0.0).then_inc(pool_const, 1)
            pool.memset(neg_half[:], -0.5).then_inc(pool_const, 1)
            pool.wait_ge(pool_const, 3)
            pool.affine_select(out=ident[:], in_=ident[:], pattern=[[-1, P]], compare_op=ALU.not_equal, fill=1.0,
                               base=0, channel_multiplier=1).then_inc(pool_const, 1)
            pool.affine_select(out=causal[:], in_=causal[:], pattern=[[-1, 2 * P]], compare_op=ALU.is_ge, fill=NEG,
                               base=P, channel_multiplier=1).then_inc(pool_const, 1)
            pool.wait_ge(pool_const, 5)
            pool.tensor_copy(ident_bf[:], ident[:]).then_inc(pool_const, 1)
            for i in range(2):
                pool.memset(vs[i][:].rearrange("p t h e -> p (t h) e")[:, :, HD:VW], 1.0).then_inc(v_ones, 1)
            pool.iota(iota[:], pattern=[[1, EXP]], base=0, channel_multiplier=0,
                      allow_small_or_imprecise_dtypes=True).then_inc(iota_ready, 1)
            pool.wait_ge(pool_const, 6)
            pool.wait_ge(v_ones, 2)
            pool.wait_ge(iota_ready, 1)
            for i in range(2):
                pool.memset(k_st[64 * i + 32:64 * i + 64].bitcast(F32), 1.0).then_inc(ones_ready, 1)
                pool.wait_ge(ones_ready, i + 1)

            def low(dst, src, high, s):
                pool.tensor_tensor(dst, src, high.bitcast(F32), ALU.subtract).then_inc(s, 1)

            def wr():
                a, b = W_CHUNKS[2]
                pool.wait_ge(w_hi[2], 1)
                low(w_l[:, a:b], w_raw[:, a:b], w_h[:, a:b], w_lo[2])

            def cut(b, g):
                pool.wait_ge(exped, SG * b + g + 1)
                v = probs[:, g, :].rearrange("p (h q) -> p h q", q=S if g < 4 else P)[:, :, 0:P]
                pool.affine_select(out=v, in_=v, pattern=[[0, 4 if g < 4 else 8], [1, P]], compare_op=ALU.is_ge,
                                   fill=0.0, base=0, channel_multiplier=-1).then_inc(cut_done, 1)

            def power(key):
                no, n = NORM_NO[key], norm_tiles(key)
                i = no % SETS
                pool.wait_ge(var_done, no + 1)
                pool.tensor_tensor(rstd[i][:, 0:n], var_eps[i][:, 0:n], neg_half[:, 0:n], ALU.pow).then_inc(rstd_done, 1)
                pool.wait_ge(neg_done, no + 1)
                pool.wait_ge(rstd_done, no + 1)
                pool.tensor_tensor(shift[i][:, 0:n], neg_mean[i][:, 0:n], rstd[i][:, 0:n], ALU.mult)\
                    .then_inc(shift_done, 1)

            def gate(b):
                pool.wait_ge(gated, b + 1)
                if b == 0:
                    pool.wait_ge(ld_vec[0], 16)
                    pool.wait_ge(ld_vec[1], 16)
                pool.tensor_tensor(gg[:, b], gb[:, b], gam_b[:].unsqueeze(1).broadcast_to([P, QT, D]), ALU.mult)\
                    .then_inc(gg_done, 1)
                pool.wait_ge(gg_done, b + 1)
                pool.tensor_tensor(gb[:, b], gb[:, b], bet_b[:].unsqueeze(1).broadcast_to([P, QT, D]), ALU.mult)\
                    .then_inc(gb_done, 1)

            def experts_lo(n):
                pool.wait_ge(ab_hi, n + 1)
                dst, high = (ea_l[:, n], ea_h[:, n]) if n < 2 else (
                    flat(v_[:, 4 * n - 8:4 * n - 4]) for v_ in (eb_l, eb_h))
                low(dst, w_raw[:, n * 1024:(n + 1) * 1024], high, ab_lo)

            def ga(tt, b):
                pool.wait_ge(y_mul, B * tt + b + 1)
                pool.tensor_tensor(gg[:, b, tt], gg[:, b, tt], gb[:, b, tt], ALU.add).then_inc(y_done, 1)

            def add_bias(q):
                pool.wait_ge(full["x2t"], q + 1)
                if q == 0:
                    pool.wait_ge(ld_vec[2], 16)
                for j in range(2):
                    b, tt = ffn_tile(2 * q + j)
                    pool.tensor_tensor(resid[:, b, tt], resid[:, b, tt], bias_b[:], ALU.add).then_inc(biased, 1)

            def pick(u):
                pool.wait_ge(routed, u + 1)
                pool.wait_ge(vc_done, u + 1)
                v = vc[u % 2][:].rearrange("p (a r) -> p a r", r=RANK)
                pool.tensor_tensor(v, v, route[u % 2][:].unsqueeze(2).broadcast_to([P, EXP, RANK]), ALU.mult)\
                    .then_inc(picked, 1)

            def spread(u):
                pool.wait_ge(v_done, u + 1)
                if u >= 2:
                    pool.wait_ge(full["zt"], u - 1)
                pool.tensor_tensor(z[u % 2][:].rearrange("p (a r) -> p a r", r=RANK),
                                   route[u % 2][:].unsqueeze(2).broadcast_to([P, EXP, RANK]),
                                   vr[u % 2][:].unsqueeze(1).broadcast_to([P, EXP, RANK]), ALU.mult).then_inc(z_done, 1)

            parts = {"wr": wr, "t": cut, "pow": lambda *key: power(key), "gate": gate, "ab": experts_lo, "ga": ga, "x2t": add_bias, "pick": pick,
                     "spread": spread}
            for step in STEPS:
                if step[0] in parts:
                    parts[step[0]](*step[1:])

        @block.vector
        def _(dve):
            count = {"added": 0, "stat": 0, "mv": 0}

            def low(dst, src, high, s):
                dve.tensor_tensor(dst, src, high.bitcast(F32), ALU.subtract).then_inc(s, 1)

            def split_lo(kind, n, dst, src, high):
                dve.wait_ge(hi[kind], n + 1)
                low(dst, src, high, lo[kind])

            def w_low(n):
                a, b = W_CHUNKS[n]
                dve.wait_ge(w_hi[n], 1)
                low(w_l[:, a:b], w_raw[:, a:b], w_h[:, a:b], w_lo[n])

            def split_x(b):
                dve.wait_ge(xT_hi, b + 1)
                low(xT_l[b % 2][:], act_raw[:, :, b * S:(b + 1) * S], xT_h[b % 2][:], xT_lo)
                if b < 2:
                    w_low(b)

            def qk(b):
                split_lo("qk", b, qk_l[:], wide("qk", b)[:].rearrange("p (m s) -> p m s", m=4), qk_h[:])

            def row_max(b, g):
                dve.wait_ge(full["s"], SG * b + g + 1)
                if g < 2:
                    dst, keys = nm[:, 0, 8 * g:8 * g + 8], P
                else:
                    dst, keys = nm[:, 1, 4 * (g - 2):4 * (g - 2) + 4], S
                if b >= 1 and g == 0:
                    dve.wait_ge(nm_lo, b)
                dve.tensor_reduce(dst, wide("s", b, g)[:].rearrange("p (h k) -> p h k", k=keys), AX.X, ALU.max,
                                  negate=True).then_inc(maxed, 1)

            def split_max(b):
                dve.wait_ge(maxed, SG * (b + 1))
                if b >= 1:
                    dve.wait_ge(full["mt"], b)
                dve.tensor_copy(nm_hl[:, :, 0, :], nm[:]).then_inc(nm_hi, 1)
                dve.wait_ge(nm_hi, b + 1)
                low(nm_hl[:, :, 1, :], nm[:], nm_hl[:, :, 0, :], nm_lo)

            def o(b):
                if b >= 1:
                    dve.wait_ge(full["at"], b)
                for t in range(QT):
                    dve.wait_ge(full["o"], 2 * b + t + 1)
                    v = narrow("o", b, t)[:].rearrange("p (h e) -> p h e", e=VW)
                    dve.reciprocal(rden[:, t, :], v[:, :, HD]).then_inc(rden_done, 1)
                    dve.wait_ge(rden_done, 2 * b + t + 1)
                    dve.tensor_tensor(attn[:, t].rearrange("p (h d) -> p h d", d=HD), v[:, :, 0:HD],
                                      rden[:, t, :].unsqueeze(2).broadcast_to([P, NH, HD]), ALU.mult)\
                       .then_inc(attn_done, 1)

            def statistics(key, tiles, eps):
                n, i = len(tiles), NORM_NO[key] % SETS
                if NORM_NO[key] >= SETS:
                    dve.wait_ge(*over(NORMS[NORM_NO[key] - SETS]))
                for j, v in enumerate(tiles):
                    dve.bn_stats(stats[i][:, j], v).then_inc(stat_done, 1)
                count["stat"] += n
                dve.wait_ge(stat_done, count["stat"])
                for j in range(n):
                    dve.bn_aggr(mv[i][:, j], stats[i][:, j]).then_inc(mv_done, 1)
                count["mv"] += n
                dve.wait_ge(mv_done, count["mv"])
                dve.tensor_scalar(var_eps[i][:, 0:n], mv[i][:, 0:n, 1], eps, None, ALU.add).then_inc(var_done, 1)
                dve.tensor_scalar(neg_mean[i][:, 0:n], mv[i][:, 0:n, 0], -1.0, None, ALU.mult).then_inc(neg_done, 1)

            def add_stats(key, psum, old):
                i, n = SUM_NO[key] % 2, norm_tiles(key)
                if SUM_NO[key] >= 2:
                    dve.wait_ge(*over(SUMS[SUM_NO[key] - 2]))
                dve.tensor_tensor(pre[i][:, 0:n], psum, old, ALU.add).then_inc(added, 1)
                count["added"] += 1
                dve.wait_ge(added, count["added"])
                statistics(key, [pre[i][:, j] for j in range(n)], 1e-5)

            def at(b):
                split_lo("at", b, flat(aT_l[:]), narrow("at", b)[:], flat(aT_h[:]))

            def n1(b):
                dve.wait_ge(full["wo"], b + 1)
                if b == 0:
                    dve.wait_ge(ld_res, 16)
                add_stats(("n1", b), narrow("wo", b)[:].rearrange("p (t d) -> p t d", t=QT), resid[:, b])

            def xt(b):
                split_lo("xt", b, flat(x1T_l[:]), narrow("xt", b)[:], flat(x1T_h[:]))

            def xq(b):
                split_lo("xq", b, xq_l[:, :, b, :], narrow("xq", b)[:].rearrange("p (h s) -> p h s", h=XH),
                         xq_h[:, :, b, :])

            def split_context(c):
                v = slice(c * 512, c * 512 + 512)
                dve.wait_ge(cT_hi, c + 1)
                low(cT_l[:, :, v], act_raw[:, :, v], cT_h[:, :, v], cT_lo)

            def xk(c):
                v = slice(c * 512, c * 512 + 512)
                split_lo("xk", c, xk_l[:, :, v], wide("xk", c)[:].rearrange("p (h s) -> p h s", h=XH), xk_h[:, :, v])

            def xv(c):
                for n in range(2):
                    b = 2 * c + n
                    split_lo("xv", b, xv_l[:, :, :, b, :],
                             wide("xv", c)[:, n * 512:n * 512 + 512].rearrange("p (t h e) -> p t h e", t=QT, h=XH),
                             xv_h[:, :, :, b, :])

            def retention_weights(h):
                if h == 0:
                    dve.wait_ge(ld_dec, 16)
                dve.wait_ge(abs_done, h + 1)
                dve.tensor_tensor(mag[:, h], mag[:, h], dec[:, h], ALU.mult).then_inc(decayed, 1)
                dve.wait_ge(decayed, h + 1)
                dve.tensor_scalar(rA_h[:, h], mag[:, h], 1.0, None, ALU.max).then_inc(rA_hi, 1)
                dve.wait_ge(rA_hi, h + 1)
                dve.scalar_tensor_tensor(out=rA_l[:, h], in0=mag[:, h], scalar=1.0, in1=rA_h[:, h].bitcast(F32),
                                         op0=ALU.max, op1=ALU.subtract).then_inc(rA_lo, 1)

            def gs(t):
                dve.wait_ge(full["ox"], t + 1)
                v = wide("ox", t)[:].rearrange("p (h b e) -> p b h e", h=XH, b=B)
                statistics(("gs", t), [v[:, b] for b in range(B)], 1e-3)

            def ga(t, b):
                dve.wait_ge(normed["gs"], B * t + b + 1)
                dve.wait_ge(gb_done, b + 1)
                dve.tensor_tensor(gg[:, b, t], gg[:, b, t], attn[:, b % 2], ALU.mult).then_inc(y_mul, 1)

            def yt(q):
                split_lo("yt", q, flat(yT_l[:]), narrow("yt", q)[:], flat(yT_h[:]))

            def n2_(q):
                t, b0 = q // 2, 2 * (q % 2)
                dve.wait_ge(full["w2"], q + 1)
                add_stats(("n2", q), narrow("w2", q)[:].rearrange("p (t d) -> p t d", t=2), resid[:, b0:b0 + 2, t])

            def x2t(q):
                split_lo("x2t", q, flat(x2T_l[:, q]), narrow("x2t", q)[:], flat(x2T_h[:, q]))

            def route_tile(u):
                dve.wait_ge(squared, u + 1)
                if u == 0:
                    dve.wait_ge(iota_ready, 1)
                dve.tensor_reduce(n2[:], sq[:].rearrange("p (a r) -> p a r", r=RANK), AX.X, ALU.add).then_inc(n2_done, 1)
                dve.wait_ge(n2_done, u + 1)
                dve.max(top[:], n2[:]).then_inc(top_done, 1)
                dve.wait_ge(top_done, u + 1)
                dve.max_index(idx[:], top[:], n2[:]).then_inc(idx_done, 1)
                dve.wait_ge(idx_done, u + 1)
                dve.tensor_tensor(eq[:], iota[:].unsqueeze(2).broadcast_to([P, EXP, TOPK]),
                                  idx[:, 0:TOPK].unsqueeze(1).broadcast_to([P, EXP, TOPK]), ALU.is_equal)\
                   .then_inc(eq_done, 1)
                dve.wait_ge(eq_done, u + 1)
                if u >= 2:
                    dve.wait_ge(z_done, u - 1)
                dve.tensor_reduce(route[u % 2][:], eq[:], AX.X, ALU.add).then_inc(routed, 1)

            def sum_picked(u):
                dve.wait_ge(picked, u + 1)
                if u >= 2:
                    dve.wait_ge(z_done, u - 1)
                dve.tensor_reduce(vr[u % 2][:], vc[u % 2][:].rearrange("p (a r) -> p r a", r=RANK), AX.X, ALU.add)\
                   .then_inc(v_done, 1)

            def zt(u):
                split_lo("zt", u, flat(zT_l[:]), wide("zt", u)[:], flat(zT_h[:]))

            def n3(u):
                b, t = ffn_tile(u)
                dve.wait_ge(full["d"], u + 1)
                dve.wait_ge(biased, u + 1)
                add_stats(("n3", u), narrow("d", u)[:, 0:D].unsqueeze(1), resid[:, b, t:t + 1])

            parts = {"xs": split_x, "qk": qk, "s": row_max, "nm": split_max, "o": o, "at": at, "n1": n1, "xt": xt,
                     "xq": xq, "cs": split_context, "xk": xk, "xv": xv, "ra": retention_weights, "gs": gs, "ga": ga,
                     "yt": yt, "n2": n2_, "x2t": x2t, "route": route_tile, "sum": sum_picked, "zt": zt, "n3": n3}
            for step in STEPS:
                if step[0] in parts:
                    parts[step[0]](*step[1:])

        @block.tensor
        def _(pe):
            def take(*key):
                if key in BEFORE:
                    pe.wait_ge(*released(BEFORE[key]))

            def three(dst, wh, wl, xh, xl, start, stop):
                pe.matmul(dst, wh, xh, start=start, stop=False)
                pe.matmul(dst, wh, xl, start=False, stop=False)
                return pe.matmul(dst, wl, xh, start=False, stop=stop)

            def qk(b):
                take("qk", b)
                pe.wait_ge(xT_lo, b + 1)
                if b == 0:
                    pe.wait_ge(w_lo[0], 1)
                for m in range(4):
                    for k in range(KD):
                        c = W_QK + k * 512 + m * P
                        mm = three(wide("qk", b)[:, m * S:(m + 1) * S], w_h[:, c:c + P], w_l[:, c:c + P],
                                   xT_h[b % 2][:, k], xT_l[b % 2][:, k], k == 0, k == KD - 1)
                mm.then_inc(full["qk"], 1)

            def by_weights(kind, n, xh, xl, col):
                take(kind, n)
                for t in range(2):
                    for k in range(KD):
                        c = col + k * D
                        mm = three(narrow(kind, n)[:, t * D:(t + 1) * D], xh[:, k, t * P:(t + 1) * P],
                                   xl[:, k, t * P:(t + 1) * P], w_h[:, c:c + D], w_l[:, c:c + D], k == 0, k == KD - 1)
                mm.then_inc(full[kind], 1)

            def v(b):
                if b == 0:
                    pe.wait_ge(w_lo[1], 1)
                by_weights("v", b, xT_h[b % 2], xT_l[b % 2], W_V)

            def s(b, g):
                take("s", b, g)
                if g == 0:
                    pe.wait_ge(stacked[b % 2], 96 * (b // 2 + 1))
                if b == 0 and g == 0:
                    pe.wait_ge(pool_const, 6)
                rows = slice(64 * (b % 2), 64 * (b % 2) + HI)
                t, heads, keys = (0, range(8 * g, 8 * g + 8), P) if g < 2 else (1, range(4 * g - 8, 4 * g - 4), S)
                n_bank = 512 // keys
                for half in range(2):
                    pe.matmul(wide("s", b, g)[:, half * 512:(half + 1) * 512].rearrange("p (h k) -> p h k", h=n_bank),
                              ident_bf[:], causal[:, 2 * P - keys:].unsqueeze(1).broadcast_to([P, n_bank, keys]),
                              start=True, stop=False)
                for n, h in enumerate(heads):
                    mm = pe.matmul(wide("s", b, g)[:, n * keys:(n + 1) * keys], q_st[rows, h, t * P:(t + 1) * P],
                                   k_st[rows, h, 0:keys], start=False, stop=n % n_bank == n_bank - 1)
                mm.then_inc(full["s"], 1)

            def mt(b):
                take("mt", b)
                pe.wait_ge(nm_lo, b + 1)
                for t in range(QT):
                    mm = pe.transpose(narrow("mt", b)[0:2 * NH, t * P:(t + 1) * P],
                                      nm_hl[:, t].rearrange("p a h -> p (a h)").bitcast(F32), ident[:])
                mm.then_inc(full["mt"], 1)

            def t(b, g):
                take("t", b, g)
                if g == 0:
                    pe.wait_ge(nm_stacked[b % 2], 16 * (b // 2 + 1))
                rows = slice(64 * (b % 2), 64 * (b % 2) + HM)
                kt, heads, q0 = (0, range(4 * g, 4 * g + 4), 0) if g < 4 else (1, range(8 * g - 32, 8 * g - 24), P)
                for n, h in enumerate(heads):
                    mm = pe.matmul(wide("t", b, g)[:, n * (S - q0):(n + 1) * (S - q0)], k_st[rows, h, kt * P:(kt + 1) * P],
                                   q_st[rows, h, q0:S], start=True, stop=True)
                mm.then_inc(full["t"], 1)

            def ot(b):
                take("ot", b)
                pe.wait_ge(v_copied, b + 1)
                pe.wait_ge(cut_done, SG * (b + 1))
                vv = vs[b % 2]
                for g in range(4):
                    for kt in range(QT):
                        for j in range(4):
                            h = 4 * g + j
                            dst = wide("ot", b)[32 * j:32 * j + 32, g * S + kt * P:(g + 1) * S]
                            if kt == 0:
                                p = probs[:, g, j * S:(j + 1) * S]
                            else:
                                p = probs[:, 4 + h // 8, (h % 8) * P:(h % 8 + 1) * P]
                            mm = pe.matmul(dst, vv[:, kt, h], p, start=(kt == 0), stop=(kt == QT - 1))
                mm.then_inc(full["ot"], 1)

            def o(b):
                pe.wait_ge(oT_copied, b + 1)
                for t in range(QT):
                    take("o", b, t)
                    for g in range(4):
                        mm = pe.transpose(narrow("o", b, t)[:, g * P:(g + 1) * P], oT[:, g, t * P:(t + 1) * P], ident[:])
                    mm.then_inc(full["o"], 1)

            def turn(kind, n, tiles):
                take(kind, n)
                for k in range(KD):
                    for t in range(2):
                        mm = pe.transpose(narrow(kind, n)[:, k * S + t * P:k * S + (t + 1) * P],
                                          tiles[t][:, k * P:(k + 1) * P], ident[:])
                mm.then_inc(full[kind], 1)

            def at(b):
                pe.wait_ge(attn_done, 2 * b + 2)
                turn("at", b, [attn[:, t] for t in range(QT)])

            def wo(b):
                pe.wait_ge(lo["at"], b + 1)
                if b == 0:
                    pe.wait_ge(w_lo[2], 1)
                by_weights("wo", b, aT_h, aT_l, W_O)

            def xt(b):
                pe.wait_ge(normed["n1"], 2 * b + 2)
                turn("xt", b, [resid[:, b, t] for t in range(QT)])

            def gate(b):
                pe.wait_ge(lo["xt"], b + 1)
                by_weights("gate", b, x1T_h, x1T_l, W_G)

            def xq(b):
                take("xq", b)
                for h in range(XH):
                    c = W_H + h * P
                    mm = three(narrow("xq", b)[:, h * S:(h + 1) * S], w_h[:, c:c + P], w_l[:, c:c + P],
                               x1T_h[:, h], x1T_l[:, h], True, True)
                mm.then_inc(full["xq"], 1)

            def xk(c):
                take("xk", c)
                pe.wait_ge(cT_lo, c + 1)
                for h in range(XH):
                    w0 = W_H + h * P
                    mm = three(wide("xk", c)[:, h * 512:(h + 1) * 512], w_h[:, w0:w0 + P], w_l[:, w0:w0 + P],
                               cT_h[:, h, c * 512:(c + 1) * 512], cT_l[:, h, c * 512:(c + 1) * 512], True, True)
                mm.then_inc(full["xk"], 1)

            def xv(c):
                take("xv", c)
                for n in range(4):
                    s0 = c * 512 + n * P
                    for h in range(XH):
                        w0 = W_H + h * P
                        mm = three(wide("xv", c)[:, n * 256 + h * P:n * 256 + (h + 1) * P], cT_h[:, h, s0:s0 + P],
                                   cT_l[:, h, s0:s0 + P], w_h[:, w0:w0 + P], w_l[:, w0:w0 + P], True, True)
                mm.then_inc(full["xv"], 1)

            def sx(h):
                take("sx", h)
                if h == 0:
                    pe.wait_ge(lo["xk"], 2)
                    pe.wait_ge(lo["xq"], B)
                for t in range(QT):
                    q0, c0 = t * P, t * S
                    for b in range(B):
                        k0 = b * S + t * P
                        mm = three(narrow("sx", h)[:, c0:c0 + S - q0], xk_h[:, h, k0:k0 + P], xk_l[:, h, k0:k0 + P],
                                   xq_h[:, h, b, q0:S], xq_l[:, h, b, q0:S], b == 0, b == B - 1)
                mm.then_inc(full["sx"], 1)

            def ox(t):
                take("ox", t)
                pe.wait_ge(lo["xv"], B)
                pe.wait_ge(ones_r_ready, 1)
                for h in range(XH):
                    pe.wait_ge(rA_lo, h + 1)
                    dst = wide("ox", t)[:, h * 512:(h + 1) * 512]
                    v0h, v0l, v1h, v1l = (v_[:, k, h].rearrange("p b e -> p (b e)") for k in range(QT) for v_ in (xv_h, xv_l))
                    three(dst, rA_h[:, h, t * P:(t + 1) * P], rA_l[:, h, t * P:(t + 1) * P], v0h, v0l, True, False)
                    if t == 0:
                        pe.matmul(dst, ones_r[:], v1h, start=False, stop=False)
                        mm = pe.matmul(dst, ones_r[:], v1l, start=False, stop=True)
                    else:
                        mm = three(dst, rA_h[:, h, 256:384], rA_l[:, h, 256:384], v1h, v1l, False, True)
                mm.then_inc(full["ox"], 1)

            def yt(q):
                t_, b0 = q // 2, 2 * (q % 2)
                pe.wait_ge(y_done, B * t_ + b0 + 2)
                turn("yt", q, [gg[:, b0 + j, t_] for j in range(2)])

            def w2(q):
                pe.wait_ge(lo["yt"], q + 1)
                by_weights("w2", q, yT_h, yT_l, W_O2)

            def x2t(q):
                t_, b0 = q // 2, 2 * (q % 2)
                pe.wait_ge(normed["n2"], 2 * q + 2)
                turn("x2t", q, [resid[:, b0 + j, t_] for j in range(2)])

            def ve(u):
                q, j = u // 2, u % 2
                take("ve", u)
                pe.wait_ge(lo["x2t"], q + 1)
                if u == 0:
                    pe.wait_ge(ab_lo, 2)
                for c in range(2):
                    for k in range(KD):
                        mm = three(wide("ve", u)[:, c * 512:(c + 1) * 512], x2T_h[:, q, k, j * P:(j + 1) * P],
                                   x2T_l[:, q, k, j * P:(j + 1) * P], ea_h[:, k, c * 512:(c + 1) * 512],
                                   ea_l[:, k, c * 512:(c + 1) * 512], k == 0, k == KD - 1)
                mm.then_inc(full["ve"], 1)

            def zt(u):
                take("zt", u)
                pe.wait_ge(z_done, u + 1)
                for k in range(ER // P):
                    mm = pe.transpose(wide("zt", u)[:, k * P:(k + 1) * P], z[u % 2][:, k * P:(k + 1) * P], ident[:])
                mm.then_inc(full["zt"], 1)

            def d(u):
                q, j = u // 2, u % 2
                take("d", u)
                dst = narrow("d", u)[:, 0:D]
                for k in range(KD):
                    c = W_F + k * D
                    three(dst, x2T_h[:, q, k, j * P:(j + 1) * P], x2T_l[:, q, k, j * P:(j + 1) * P],
                          w_h[:, c:c + D], w_l[:, c:c + D], k == 0, False)
                pe.wait_ge(lo["zt"], u + 1)
                if u == 0:
                    pe.wait_ge(ab_lo, 4)
                for k in range(ER // P):
                    mm = three(dst, zT_h[:, k], zT_l[:, k], eb_h[:, k], eb_l[:, k], False, k == ER // P - 1)
                mm.then_inc(full["d"], 1)

            parts = {"qk": qk, "v": v, "s": s, "mt": mt, "t": t, "ot": ot, "o": o, "at": at, "wo": wo, "xt": xt,
                     "gate": gate, "xq": xq, "xk": xk, "xv": xv, "sx": sx, "ox": ox, "yt": yt, "w2": w2, "x2t": x2t,
                     "ve": ve, "zt": zt, "d": d}
            for step in STEPS:
                if step[0] in parts:
                    parts[step[0]](*step[1:])


def _decay():
    import numpy as np
    idx = np.arange(S, dtype=np.float32)
    out = np.zeros((P, XH, 384), np.float32)
    for h in range(XH):
        gam = np.float64(1.0 - 2.0 ** (-5.0 - h))
        expo = idx[None, :] - idx[:, None]
        d = np.where(expo <= 0, gam ** np.minimum(expo, 0), 0.0)
        d = (d / np.sqrt(d.sum(-1))[None, :] / np.sqrt(128.0)).T.astype(np.float32)
        out[:, h, 0:S] = d[0:P]
        out[:, h, S:] = d[P:, P:]
    return out


def kernel(x, ctx_2048, L0_attn_w_qkv, L0_attn_w_o, L0_xattn_Wh, L0_xattn_wg_w, L0_xattn_wo_w, L0_xattn_gn_gamma,
           L0_xattn_gn_beta, L0_ffn_A, L0_ffn_B, L0_ffn_W, L0_ffn_bias):
    import numpy as np
    import concourse.bacc as bacc
    from concourse.bass_utils import run_bass_kernel_spmd

    def rows(a):
        a = np.asarray(a)
        return a.reshape(a.shape[0] // P, P, a.shape[1]).transpose(1, 0, 2)

    def flat(a):
        return a.reshape(P, -1)

    def heads(a):
        return np.asarray(a).reshape(HB, 2, HD, D).transpose(1, 2, 0, 3).reshape(D, D)

    wqkv = np.asarray(L0_attn_w_qkv)
    wqk = np.concatenate([heads(wqkv[0:D]), heads(wqkv[D:2 * D])], 0)
    w = np.concatenate([flat(rows(wqk.T)), flat(rows(wqkv[2 * D:].T)), flat(rows(np.asarray(L0_attn_w_o).T)),
                        flat(np.asarray(L0_xattn_Wh).transpose(1, 0, 2)), flat(rows(L0_xattn_wg_w)),
                        flat(rows(L0_xattn_wo_w)), flat(rows(np.asarray(L0_ffn_W).T))], 1)
    a = np.asarray(L0_ffn_A).reshape(ER, D).T
    b = np.asarray(L0_ffn_B).transpose(0, 2, 1).reshape(ER, D)
    xf, cf = np.asarray(x).reshape(B * S, D), np.asarray(ctx_2048).reshape(B * S, D)
    arrays = {
        "x": np.asarray(x).reshape(B, QT, P, D).transpose(2, 0, 1, 3),
        "xT": rows(xf.T), "cT": rows(cf.T), "w": w, "aT": flat(rows(a)), "bT": flat(rows(b)),
        "gam": np.broadcast_to(np.asarray(L0_xattn_gn_gamma), (P, D)),
        "bet": np.broadcast_to(np.asarray(L0_xattn_gn_beta), (P, D)),
        "bias": np.broadcast_to(np.asarray(L0_ffn_bias), (P, D)),
        "decay": _decay(),
    }
    arrays = {k + "_dram": np.ascontiguousarray(v) for k, v in arrays.items()}
    nc = bacc.Bacc("TRN2", target_bir_lowering=False, num_devices=1)
    args = [nc.dram_tensor(k, v.shape, mybir.dt.from_np(v.dtype), kind="ExternalInput").ap() for k, v in arrays.items()]
    args.append(nc.dram_tensor("out_dram", (P, B, QT, D), F32, kind="ExternalOutput").ap())
    decoder_layer(nc, *args)
    r = run_bass_kernel_spmd(nc, [arrays], core_ids=[0])
    got = r.results[0]["out_dram"]
    return np.ascontiguousarray(got.transpose(1, 2, 0, 3).reshape(B, S, D))
```

```python
from contextlib import ExitStack

import concourse.bass as bass
from concourse import mybir

F32 = mybir.dt.float32
F32R = mybir.dt.float32r
BF16 = mybir.dt.bfloat16
U32 = mybir.dt.uint32
ALU = mybir.AluOpType
ACT = mybir.ActivationFunctionType
AX = mybir.AxisListType

P = 128
B, S, D = 4, 256, 256
KD = D // P
QT = S // P
NH, HD = 16, 16
XH = 2
EXP, RANK, TOPK = 64, 16, 4
ER = EXP * RANK
NEG = -3.0e38
HI = 3 * HD
HM = HI + 2
HB = 8
SG = 6

W_QK, W_V, W_O, W_H, W_G, W_O2, W_F = 0, 1024, 1536, 2048, 2304, 2816, 3328
W_N = 3840
W_CHUNKS = ((W_QK, W_QK + 512), (W_QK + 512, W_V), (W_V, W_O), (W_O, W_N))
VW = 32
FFN_TILES = B * QT
WARM = 8


def ffn_tile(u):
    q = u // 2
    return 2 * (q % 2) + u % 2, q // 2


ORDER = (
    "xs:0 ws:0 ws:1 qk:0 ws:2 xs:1 stack:0 v:0 qk:1 "
    "s:0:0 s:0:1 s:0:2 lr s:0:3 xs:2 s:0:4 s:0:5 stack:1 nm:0 ws:3 qk:2 mt:0 s:1:0 s:1:1 s:1:2 v:1 "
    "t:0:0 s:1:3 t:0:1 t:0:2 s:1:4 t:0:3 s:1:5 t:0:4 t:0:5 le nm:1 mt:1 v:2 ot:0 xs:3 "
    "t:1:0 t:1:1 o:0 s:2:0 s:2:1 stack:2 t:1:2 s:2:2 at:0 t:1:3 s:2:3 lc s:2:4 t:1:4 pow:n1:0 s:2:5 n1:0 wo:0 "
    "nm:2 norm:n1:0 t:1:5 qk:3 mt:2 xt:0 ot:1 "
    "t:2:0 t:2:1 o:1 t:2:2 xq:0 at:1 t:2:3 s:3:0 s:3:1 s:3:2 t:2:4 gate:0 s:3:3 s:3:4 t:2:5 s:3:5 nm:3 v:3 "
    "pow:n1:1 stack:3 wo:1 mt:3 n1:1 ot:2 norm:n1:1 xt:1 "
    "t:3:0 t:3:1 o:2 t:3:2 t:3:3 at:2 t:3:4 xq:1 t:3:5 pow:n1:2 n1:2 wo:2 norm:n1:2 gate:1 "
    "ot:3 xt:2 o:3 cs:0 at:3 cs:1 xq:2 n1:3 xk:0 wo:3 norm:n1:3 pow:n1:3 xk:1 gate:2 xt:3 xv:0 xq:3 xv:1 "
    "sx:0 sx:1 ra:0 gate:3 ox:0 ra:1 gs:0 ox:1 gm:0 pow:gs:0 pow:gs:1 ga:0 gs:1 "
    "yt:0 ab:0 gm:1 ab:1 yt:1 ga:1 n2:0 pow:n2:0 ab:2 w2:0 yt:2 norm:n2:0 w2:1 n2:1 x2t:0 pow:n2:1 norm:n2:1 "
    "w2:2 ab:3 n2:2 pick:0 pow:n2:2 spread:0 pick:1 yt:3 route:0 "
    "ve:0 n2:3 spread:1 w2:3 pick:2 sum:0 x2t:1 route:1 ve:1 db:0 pow:n2:3 zt:0 sum:1 norm:n2:2 spread:2 "
    "route:2 n3:0 ve:2 x2t:2 d:0 pick:3 zt:1 ve:3 pow:n3:0 db:1 sum:2 norm:n2:3 d:1 route:3 n3:1 zt:2 "
    "pow:n3:1 sum:3 norm:n3:0 ve:4 route:4 db:2 spread:3 x2t:3 pick:4 d:2 n3:2 zt:3 ve:5 sum:4 pow:n3:2 db:3 "
    "norm:n3:1 norm:n3:2 d:3 spread:4 route:5 n3:3 zt:4 sum:5 ve:6 pick:5 route:6 ve:7 spread:5 route:7 "
    "pow:n3:3 zt:5 db:4 sum:6 d:4 sum:7 norm:n3:3 n3:4 db:5 pick:6 n3:5 d:5 pick:7 zt:6 db:6 norm:n3:4 "
    "spread:6 zt:7 spread:7 pow:n3:4 db:7 pow:n3:5 n3:6 d:6 pow:n3:6 norm:n3:5 pow:n3:7 d:7 n3:7 norm:n3:6 "
    "norm:n3:7 "
)
STEPS = [tuple(int(v) if v.isdigit() else v for v in step.split(":")) for step in ORDER.split()]
WIDE_SLOTS, NARROW_SLOTS = 3, 2
WIDE = [k for k in STEPS if k[0] in ("qk", "s", "t", "ot", "xk", "xv", "ox", "ve", "zt")]
NARROW = [k for step in STEPS for k in ([("o", step[1], t) for t in range(QT)] if step[0] == "o" else [step])
          if k[0] in ("v", "mt", "o", "at", "wo", "xt", "gate", "xq", "sx", "yt", "w2", "x2t", "db")]
SLOT = {k: n % WIDE_SLOTS for n, k in enumerate(WIDE)}
SLOT.update({k: n % NARROW_SLOTS for n, k in enumerate(NARROW)})
BEFORE = {k: WIDE[n - WIDE_SLOTS] for n, k in enumerate(WIDE) if n >= WIDE_SLOTS}
BEFORE.update({k: NARROW[n - NARROW_SLOTS] for n, k in enumerate(NARROW) if n >= NARROW_SLOTS})
NORMS = [k for k in STEPS if k[0] in ("n1", "gs", "n2", "n3")]
NORM_NO = {k: n for n, k in enumerate(NORMS)}
SETS = 3
ACT_NORMS = {("n2", 2), ("n3", 3)}
SUMS = [k for k in NORMS if k[0] != "gs"]
SUM_NO = {k: n for n, k in enumerate(SUMS)}


def decoder_layer(nc, x, xT, cT, w, aT, bT, gam, bet, bias, decay, out):
    with ExitStack() as ctx:
        def sb(name, shape, dt=F32, stack=ctx):
            return stack.enter_context(nc.sbuf_tensor(name, shape, dt))

        def sem(name):
            return ctx.enter_context(nc.semaphore(name))

        ident = sb("ident", [P, P])
        ident_bf = sb("ident_bf", [P, P], BF16)
        causal = sb("causal", [P, P], BF16)
        iota = sb("iota", [P, EXP])
        neg_half = sb("neg_half", [P, 4])
        w_raw = sb("w_raw", [P, 4096])
        w_h = sb("w_h", [P, W_N], F32R)
        w_l = sb("w_l", [P, W_N], F32R)
        resid = sb("resid", [P, B, QT, D])
        act_raw = sb("act_raw", [P, KD, B * S])
        x1T_h = sb("x1T_h", [P, KD, S], F32R)
        x1T_l = sb("x1T_l", [P, KD, S], F32R)
        xq_h = sb("xq_h", [P, XH, B, S], F32R)
        xq_l = sb("xq_l", [P, XH, B, S], F32R)
        gb = sb("gb", [P, B, QT, D])
        gg = sb("gg", [P, B, QT, D])
        gam_b = sb("gam_b", [P, D])
        bet_b = sb("bet_b", [P, D])
        bias_b = sb("bias_b", [P, D])
        pre = [sb(f"pre{i}", [P, 2, D]) for i in range(2)]
        stats = [sb(f"stats{i}", [P, 4, 6]) for i in range(SETS)]
        mv = [sb(f"mv{i}", [P, 4, 2]) for i in range(SETS)]
        var_eps = [sb(f"var_eps{i}", [P, 4]) for i in range(SETS)]
        neg_mean = [sb(f"neg_mean{i}", [P, 4]) for i in range(SETS)]
        shift = [sb(f"shift{i}", [P, 4]) for i in range(SETS)]
        rstd = [sb(f"rstd{i}", [P, 4]) for i in range(SETS)]
        rden = sb("rden", [P, QT, NH])
        attn = sb("attn", [P, QT, D])
        aT_h = sb("aT_h", [P, KD, S], F32R)
        aT_l = sb("aT_l", [P, KD, S], F32R)
        att = ExitStack()
        xT_h = [sb(f"xT_h{i}", [P, KD, S], F32R, att) for i in range(2)]
        xT_l = [sb(f"xT_l{i}", [P, KD, S], F32R, att) for i in range(2)]
        qk_h = sb("qk_h", [P, 4, S], F32R, att)
        qk_l = sb("qk_l", [P, 4, S], F32R, att)
        q_st = sb("q_st", [P, NH, S], F32R, att)
        k_st = sb("k_st", [P, NH, S], F32R, att)
        vs = [sb(f"vs{i}", [P, QT, NH, VW], F32, att) for i in range(2)]
        probs = sb("probs", [P, SG, 1024], F32, att)
        nm = sb("nm", [P, QT, NH], F32, att)
        nm_hl = sb("nm_hl", [P, QT, 2, NH], F32R, att)
        nmT = sb("nmT", [2 * NH, S], F32R, att)
        oT = sb("oT", [P, 4, S], F32, att)
        att.close()
        ea_h = sb("ea_h", [P, KD, ER], F32R)
        ea_l = sb("ea_l", [P, KD, ER], F32R)
        eb_h = sb("eb_h", [P, ER // P, D], F32R)
        eb_l = sb("eb_l", [P, ER // P, D], F32R)
        yT_h, yT_l = (aT_h, x1T_h), (aT_l, x1T_l)
        ret = ExitStack()
        cT_h = sb("cT_h", [P, KD, B * S], F32R, ret)
        cT_l = sb("cT_l", [P, KD, B * S], F32R, ret)
        xk_h = sb("xk_h", [P, XH, B * S], F32R, ret)
        xk_l = sb("xk_l", [P, XH, B * S], F32R, ret)
        xv_h = sb("xv_h", [P, QT, XH, B, P], F32R, ret)
        xv_l = sb("xv_l", [P, QT, XH, B, P], F32R, ret)
        dec = sb("dec", [P, XH, 384], F32, ret)
        mag = sb("mag", [P, XH, 384], F32, ret)
        rA_h = sb("rA_h", [P, XH, 384], F32R, ret)
        rA_l = sb("rA_l", [P, XH, 384], F32R, ret)
        ones_r = sb("ones_r", [P, P], F32R, ret)
        ret.close()
        x2T_h = sb("x2T_h", [P, 4, KD, S], F32R)
        x2T_l = sb("x2T_l", [P, 4, KD, S], F32R)
        sq = sb("sq", [P, ER])
        vc = [sb(f"vc{i}", [P, ER]) for i in range(2)]
        n2 = sb("n2", [P, EXP])
        top = sb("top", [P, 8])
        idx = sb("idx", [P, 8], U32)
        eq = sb("eq", [P, EXP, TOPK])
        route = [sb(f"route{i}", [P, EXP]) for i in range(2)]
        vr = [sb(f"vr{i}", [P, RANK]) for i in range(2)]
        z = [sb(f"z{i}", [P, ER]) for i in range(2)]
        zT_h = [sb(f"zT_h{i}", [P, ER // P, P], F32R) for i in range(2)]
        zT_l = [sb(f"zT_l{i}", [P, ER // P, P], F32R) for i in range(2)]
        res = [sb(f"res{i}", [P, D]) for i in range(2)]

        wide_ps = [ctx.enter_context(nc.psum_tensor(f"wide{i}", [P, 1024], F32)) for i in range(WIDE_SLOTS)]
        narrow_ps = [ctx.enter_context(nc.psum_tensor(f"narrow{i}", [P, 512], F32)) for i in range(NARROW_SLOTS)]

        def wide(*key):
            return wide_ps[SLOT[key]]

        def narrow(*key):
            return narrow_ps[SLOT[key]]

        def flat(v):
            return v.rearrange("p k s -> p (k s)")

        ld_x = [sem(f"ld_x{b}") for b in range(B)]
        ld_w = [sem(f"ld_w{n}") for n in range(4)]
        ld_c, ld_res, ld_a, ld_b, ld_dec = (sem(n) for n in ("ld_c", "ld_res", "ld_a", "ld_b", "ld_dec"))
        ld_vec = [sem(f"ld_vec{n}") for n in range(3)]
        stacked = [sem(f"stacked{i}") for i in range(2)]
        nm_stacked = [sem(f"nm_stacked{i}") for i in range(2)]
        stored = [sem(f"stored{i}") for i in range(2)]
        pool_const, iota_ready, ones_ready, v_ones, ones_r_ready = (
            sem(n) for n in ("pool_const", "iota_ready", "ones_ready", "v_ones", "ones_r_ready"))
        w_hi = [sem(f"w_hi{n}") for n in range(4)]
        w_lo = [sem(f"w_lo{n}") for n in range(4)]
        xT_hi, xT_lo, cT_hi, cT_lo, ab_hi, ab_lo = (sem(n) for n in ("xT_hi", "xT_lo", "cT_hi", "cT_lo", "ab_hi", "ab_lo"))
        full = {k: sem("pe_" + k) for k in ("qk", "v", "s", "mt", "t", "ot", "o", "at", "wo", "xt", "gate", "xq", "xk",
                                            "xv", "sx", "ox", "yt", "w2", "x2t", "ve", "zt", "d")}
        hi = {k: sem(k + "_hi") for k in ("qk", "at", "xt", "xq", "xk", "xv", "yt", "x2t", "zt")}
        lo = {k: sem(k + "_lo") for k in ("qk", "at", "xt", "xq", "xk", "xv", "yt", "x2t", "zt")}
        v_copied, maxed, nm_hi, nm_lo, nmT_copied, exped, cut_done, oT_copied, rden_done, attn_done = (
            sem(n) for n in ("v_copied", "maxed", "nm_hi", "nm_lo", "nmT_copied", "exped", "cut_done", "oT_copied",
                             "rden_done", "attn_done"))
        gated, gg_done, gb_done, keys_copied = (sem(n) for n in ("gated", "gg_done", "gb_done", "keys_copied"))
        added, stat_done, mv_done, var_done, rstd_done = (sem(n) for n in (
            "added", "stat_done", "mv_done", "var_done", "rstd_done"))
        neg_done, shift_done = sem("neg_done"), sem("shift_done")
        norm_sem = {(k, e): sem(f"normed_{k}_{e}") for k in ("n1", "n2", "n3") for e in ("dve", "act")
                    if any(q[0] == k and (q in ACT_NORMS) == (e == "act") for q in NORMS)}
        abs_done, decayed, rA_hi, rA_lo, y_mul, y_done = (sem(n) for n in (
            "abs_done", "decayed", "rA_hi", "rA_lo", "y_mul", "y_done"))
        squared, vc_done, n2_done, top_done, idx_done, eq_done, routed = (sem(n) for n in (
            "squared", "vc_done", "n2_done", "top_done", "idx_done", "eq_done", "routed"))
        picked, v_done, z_done, biased = (sem(n) for n in ("picked", "v_done", "z_done", "biased"))

        def released(key):
            k, n = key[0], key[1:]
            if k in ("qk", "at", "xt", "xq", "xk", "yt", "x2t", "zt"):
                return lo[k], n[0] + 1
            if k in ("wo", "w2", "db"):
                return added, SUM_NO[{"wo": "n1", "w2": "n2", "db": "n3"}[k], n[0]] + 1
            return {
                "xv": lambda: (lo["xv"], 2 * n[0] + 2),
                "v": lambda: (v_copied, n[0] + 1),
                "s": lambda: (maxed, SG * n[0] + n[1] + 1),
                "mt": lambda: (nmT_copied, n[0] + 1),
                "t": lambda: (exped, SG * n[0] + n[1] + 1),
                "ot": lambda: (oT_copied, n[0] + 1),
                "o": lambda: (attn_done, QT * n[0] + n[1] + 1),
                "gate": lambda: (gated, n[0] + 1),
                "sx": lambda: (abs_done, n[0] + 1),
                "ox": lambda: (y_mul, B * n[0] + B),
                "ve": lambda: (vc_done, n[0] + 1),
            }[k]()

        def norm_tiles(key):
            return {"n1": 2, "gs": 4, "n2": 2, "n3": 1}[key[0]]

        def over(key):
            if key[0] == "gs":
                return y_done, norm_tiles(key) * (key[1] + 1)
            by_act = key in ACT_NORMS
            steps = [m for m in range(key[1] + 1) if ((key[0], m) in ACT_NORMS) == by_act]
            return norm_sem[key[0], "act" if by_act else "dve"], norm_tiles(key) * len(steps)

        def act_norm_no(key):
            return sum(q in ACT_NORMS for q in NORMS[:NORM_NO[key] + 1])

        def norm_ends(kind, n):
            src = pre[SUM_NO[kind, n] % 2]
            if kind == "n1":
                return [(src[:, j], resid[:, n, j]) for j in range(2)]
            if kind == "n2":
                return [(src[:, j], resid[:, b, tt]) for j in range(2) for b, tt in (ffn_tile(2 * n + j),)]
            return [(src[:, 0], res[n % 2][:])]

        block = ctx.enter_context(nc.Block())

        @block.sync
        def _(sp):
            def load_x(b):
                sp.dma_start(act_raw[:, :, b * S:(b + 1) * S], xT[:, :, b * S:(b + 1) * S]).then_inc(ld_x[b], 16)

            def load_w(n):
                a, b = W_CHUNKS[n]
                sp.dma_start(w_raw[:, a:b], w[:, a:b]).then_inc(ld_w[n], 16)

            load_x(0)
            for n in range(3):
                load_w(n)
            for b in range(1, B):
                load_x(b)

            def stack_scores(b):
                sp.wait_ge(hi["qk"], b + 1)
                if b < 2:
                    sp.wait_ge(ones_ready, b + 1)
                else:
                    sp.wait_ge(full["t"], SG * (b - 1))
                base, signal = 64 * (b % 2), stacked[b % 2]
                for n, (stack, part) in enumerate(((q_st, qk_h[:, 0:2]), (k_st, qk_h[:, 2:4]), (q_st, qk_h[:, 0:2]),
                                                   (k_st, qk_h[:, 2:4]), (k_st, qk_l[:, 2:4]), (q_st, qk_l[:, 0:2]))):
                    if n == 4:
                        sp.wait_ge(lo["qk"], b + 1)
                    row = base + HD * (0, 0, 1, 2, 1, 2)[n]
                    sp.dma_start(stack[row:row + HD].bitcast(F32), part.bitcast(F32)).then_inc(signal, 16)

            def stack_max(b):
                sp.wait_ge(nmT_copied, b + 1)
                if b >= 2:
                    sp.wait_ge(full["t"], SG * (b - 1))
                row = 64 * (b % 2) + HI
                sp.dma_start(q_st[row:row + 2].bitcast(F32), nmT[:].bitcast(F32)).then_inc(nm_stacked[b % 2], 16)

            def load_rest():
                load_w(3)
                for n, (dst, src) in enumerate(((gam_b, gam), (bet_b, bet), (bias_b, bias))):
                    sp.dma_start(dst[:], src).then_inc(ld_vec[n], 16)
                sp.dma_start(resid[:], x).then_inc(ld_res, 16)

            def load_experts():
                for n in range(4):
                    sp.wait_ge(w_lo[n], 1)
                sp.dma_start(w_raw[:, 0:2048], aT).then_inc(ld_a, 16)
                sp.dma_start(w_raw[:, 2048:4096], bT).then_inc(ld_b, 16)

            def load_context():
                sp.wait_ge(xT_lo, B)
                sp.dma_start(act_raw[:], cT).then_inc(ld_c, 16)

            def load_decay():
                sp.wait_ge(full["o"], 2 * B)
                sp.dma_start(dec[:], decay).then_inc(ld_dec, 16)

            def store(u):
                b, t = ffn_tile(u)
                sp.wait_ge(*over(("n3", u)))
                sp.dma_start(out[:, b, t, :], res[u % 2][:]).then_inc(stored[u % 2], 16)

            for step in STEPS:
                k, n = step[0], step[1:]
                if k == "stack":
                    stack_scores(*n)
                elif k == "lr":
                    load_rest()
                elif k == "le":
                    load_experts()
                elif k == "lc":
                    load_context()
                elif k == "mt":
                    stack_max(*n)
                elif step == ("cs", 0):
                    load_decay()
                elif k == "norm" and n[0] == "n3":
                    store(n[1])
            for i in range(2):
                sp.wait_ge(stored[i], 16 * (FFN_TILES // 2))

        @block.scalar
        def _(act):
            act.wait_ge(pool_const, 3)
            act.activation(var_eps[0][:], neg_half[:], ACT.Copy)

            def w_split(n):
                a, b = W_CHUNKS[n]
                act.wait_ge(ld_w[n], 16)
                act.activation(w_h[:, a:b], w_raw[:, a:b], ACT.Copy).then_inc(w_hi[n], 1)

            def split_x(b):
                act.wait_ge(ld_x[b], 16)
                if b >= 2:
                    act.wait_ge(full["qk"], b - 1)
                    act.wait_ge(full["v"], b - 1)
                act.activation(xT_h[b % 2][:], act_raw[:, :, b * S:(b + 1) * S], ACT.Copy).then_inc(xT_hi, 1)

            def split_hi(kind, n, dst, src):
                act.wait_ge(full[kind], n + 1)
                act.activation(dst, src, ACT.Copy).then_inc(hi[kind], 1)

            def qk(b):
                if b >= 1:
                    act.wait_ge(stacked[(b - 1) % 2], 96 * ((b - 1) // 2 + 1))
                split_hi("qk", b, qk_h[:], wide("qk", b)[:].rearrange("p (m s) -> p m s", m=4))

            def v(b):
                act.wait_ge(full["v"], b + 1)
                if b < 2:
                    act.wait_ge(v_ones, b + 1)
                else:
                    act.wait_ge(full["ot"], b - 1)
                act.activation(vs[b % 2][:].rearrange("p t h e -> p (t h) e")[:, :, 0:HD],
                               narrow("v", b)[:].rearrange("p (n d) -> p n d", d=HD), ACT.Copy)\
                   .then_inc(v_copied, 1)

            def mt(b):
                act.wait_ge(full["mt"], b + 1)
                if b >= 1:
                    act.wait_ge(nm_stacked[(b - 1) % 2], 16 * ((b - 1) // 2 + 1))
                act.activation(nmT[:], narrow("mt", b)[0:2 * NH, 0:S], ACT.Copy).then_inc(nmT_copied, 1)

            def t(b, g):
                act.wait_ge(full["t"], SG * b + g + 1)
                if b >= 1:
                    act.wait_ge(full["ot"], b)
                act.activation(probs[:, g, :], wide("t", b, g)[:], ACT.Exp, scale=HD ** -0.5).then_inc(exped, 1)

            def ot(b):
                act.wait_ge(full["ot"], b + 1)
                if b >= 1:
                    act.wait_ge(full["o"], 2 * b)
                act.activation(flat(oT[:]), wide("ot", b)[:], ACT.Copy).then_inc(oT_copied, 1)

            def at(b):
                if b >= 1:
                    act.wait_ge(full["wo"], b)
                split_hi("at", b, flat(aT_h[:]), narrow("at", b)[:])

            def xt(b):
                if b >= 1:
                    act.wait_ge(full["gate"], b)
                split_hi("xt", b, flat(x1T_h[:]), narrow("xt", b)[:])

            def gate(b):
                act.wait_ge(full["gate"], b + 1)
                act.activation(flat(gb[:, b]), narrow("gate", b)[:], ACT.Relu).then_inc(gated, 1)

            def xq(b):
                split_hi("xq", b, xq_h[:, :, b, :], narrow("xq", b)[:].rearrange("p (h s) -> p h s", h=XH))

            def split_context(c):
                if c == 0:
                    act.wait_ge(ld_c, 16)
                    act.wait_ge(full["o"], 2 * B)
                    act.activation(ones_r[:], ident[:], ACT.Copy, scale=0.0, bias=1.0).then_inc(ones_r_ready, 1)
                v_ = slice(c * 512, c * 512 + 512)
                act.activation(cT_h[:, :, v_], act_raw[:, :, v_], ACT.Copy).then_inc(cT_hi, 1)

            def xk(c):
                act.wait_ge(full["xk"], c + 1)
                act.wait_ge(cT_lo, c + 1)
                keys = wide("xk", c)[:].rearrange("p (h s) -> p h s", h=XH)
                act.activation(act_raw[:, :, c * 512:c * 512 + 512], keys, ACT.Copy).then_inc(keys_copied, 1)
                split_hi("xk", c, xk_h[:, :, c * 512:c * 512 + 512], keys)

            def xv(c):
                act.wait_ge(full["xv"], c + 1)
                for n in range(2):
                    act.activation(xv_h[:, :, :, 2 * c + n, :],
                                   wide("xv", c)[:, n * 512:n * 512 + 512].rearrange("p (t h e) -> p t h e", t=QT, h=XH),
                                   ACT.Copy).then_inc(hi["xv"], 1)

            def experts_hi(n):
                act.wait_ge((ld_a, ld_b)[n // 2], 16)
                dst = ea_h[:, n] if n < 2 else flat(eb_h[:, 4 * n - 8:4 * n - 4])
                act.activation(dst, w_raw[:, n * 1024:(n + 1) * 1024], ACT.Copy).then_inc(ab_hi, 1)

            def sx(h):
                act.wait_ge(full["sx"], h + 1)
                act.activation(mag[:, h], narrow("sx", h)[:, 0:384], ACT.Abs).then_inc(abs_done, 1)

            def norm(kind, n):
                if (kind, n) not in ACT_NORMS:
                    return
                i = NORM_NO[kind, n] % SETS
                act.wait_ge(shift_done, act_norm_no((kind, n)))
                if kind == "n3" and n >= 2:
                    act.wait_ge(stored[n % 2], 16 * (n // 2))
                for j, (src, dst) in enumerate(norm_ends(kind, n)):
                    act.activation(dst, src, ACT.Identity, bias=shift[i][:, j:j + 1], scale=rstd[i][:, j:j + 1])\
                       .then_inc(norm_sem[kind, "act"], 1)

            def yt(q):
                if q >= 2:
                    act.wait_ge(full["w2"], q - 1)
                split_hi("yt", q, flat(yT_h[q % 2][:]), narrow("yt", q)[:])

            def x2t(q):
                act.wait_ge(full["ox"], 2)
                split_hi("x2t", q, flat(x2T_h[:, q]), narrow("x2t", q)[:])

            def ve(u):
                act.wait_ge(full["ve"], u + 1)
                if u >= 1:
                    act.wait_ge(n2_done, u)
                act.activation(sq[:], wide("ve", u)[:], ACT.Square).then_inc(squared, 1)
                if u >= 2:
                    act.wait_ge(v_done, u - 1)
                act.activation(vc[u % 2][:], wide("ve", u)[:], ACT.Copy, scale=1.0 / TOPK ** 2).then_inc(vc_done, 1)

            def zt(u):
                if u >= 2:
                    act.wait_ge(full["d"], u - 1)
                split_hi("zt", u, flat(zT_h[u % 2][:]), wide("zt", u)[:])

            parts = {"xs": split_x, "ws": w_split, "qk": qk, "v": v, "mt": mt, "t": t, "ot": ot, "at": at,
                     "xt": xt, "gate": gate, "xq": xq, "cs": split_context, "xk": xk, "xv": xv,
                     "ab": experts_hi, "sx": sx, "norm": norm, "yt": yt, "x2t": x2t, "ve": ve, "zt": zt}
            for step in STEPS:
                if step[0] in parts:
                    parts[step[0]](*step[1:])

        @block.gpsimd
        def _(pool):
            pool.memset(ident[:], 0.0).then_inc(pool_const, 1)
            pool.memset(causal[:], 0.0).then_inc(pool_const, 1)
            pool.memset(neg_half[:], -0.5).then_inc(pool_const, 1)
            pool.wait_ge(pool_const, 3)
            pool.affine_select(out=ident[:], in_=ident[:], pattern=[[-1, P]], compare_op=ALU.not_equal, fill=1.0,
                               base=0, channel_multiplier=1).then_inc(pool_const, 1)
            pool.affine_select(out=causal[:], in_=causal[:], pattern=[[-1, P]], compare_op=ALU.is_ge, fill=NEG,
                               base=0, channel_multiplier=1).then_inc(pool_const, 1)
            pool.wait_ge(pool_const, 5)
            pool.tensor_copy(ident_bf[:], ident[:]).then_inc(pool_const, 1)
            pool.wait_ge(pool_const, 6)
            for i in range(2):
                pool.memset(k_st[64 * i + 32:64 * i + 64].bitcast(F32), 1.0).then_inc(ones_ready, 1)
                pool.wait_ge(ones_ready, i + 1)
            for i in range(2):
                pool.memset(vs[i][:].rearrange("p t h e -> p (t h) e")[:, :, HD:VW], 1.0).then_inc(v_ones, 1)
            pool.iota(iota[:], pattern=[[1, EXP]], base=0, channel_multiplier=0,
                      allow_small_or_imprecise_dtypes=True).then_inc(iota_ready, 1)

            def low(dst, src, high, s):
                pool.tensor_tensor(dst, src, high.bitcast(F32), ALU.subtract).then_inc(s, 1)

            def w_low(n):
                if n == 3:
                    a, b = W_CHUNKS[n]
                    pool.wait_ge(w_hi[n], 1)
                    low(w_l[:, a:b], w_raw[:, a:b], w_h[:, a:b], w_lo[n])

            def cut(b, g):
                pool.wait_ge(exped, SG * b + g + 1)
                v = probs[:, g, :].rearrange("p (h q) -> p h q", q=S if g < 4 else P)[:, :, 0:P]
                pool.affine_select(out=v, in_=v, pattern=[[0, 4 if g < 4 else 8], [1, P]], compare_op=ALU.is_ge,
                                   fill=0.0, base=0, channel_multiplier=-1).then_inc(cut_done, 1)

            def power(*key):
                i, n = NORM_NO[key] % SETS, norm_tiles(key)
                pool.wait_ge(var_done, NORM_NO[key] + 1)
                pool.tensor_tensor(rstd[i][:, 0:n], var_eps[i][:, 0:n], neg_half[:, 0:n], ALU.pow).then_inc(rstd_done, 1)
                if key in ACT_NORMS:
                    pool.wait_ge(rstd_done, NORM_NO[key] + 1)
                    pool.wait_ge(neg_done, act_norm_no(key))
                    pool.tensor_tensor(shift[i][:, 0:n], neg_mean[i][:, 0:n], rstd[i][:, 0:n], ALU.mult)\
                        .then_inc(shift_done, 1)

            def gate(b):
                pool.wait_ge(gated, b + 1)
                if b == 0:
                    pool.wait_ge(ld_vec[0], 16)
                    pool.wait_ge(ld_vec[1], 16)
                pool.tensor_tensor(gg[:, b], gb[:, b], gam_b[:].unsqueeze(1).broadcast_to([P, QT, D]), ALU.mult)\
                    .then_inc(gg_done, 1)
                pool.wait_ge(gg_done, b + 1)
                pool.tensor_tensor(gb[:, b], gb[:, b], bet_b[:].unsqueeze(1).broadcast_to([P, QT, D]), ALU.mult)\
                    .then_inc(gb_done, 1)

            def experts_lo(n):
                pool.wait_ge(ab_hi, n + 1)
                dst, high = (ea_l[:, n], ea_h[:, n]) if n < 2 else (
                    flat(v_[:, 4 * n - 8:4 * n - 4]) for v_ in (eb_l, eb_h))
                low(dst, w_raw[:, n * 1024:(n + 1) * 1024], high, ab_lo)

            def add_bias(q):
                pool.wait_ge(full["x2t"], q + 1)
                if q == 0:
                    pool.wait_ge(ld_vec[2], 16)
                for j in range(2):
                    b, tt = ffn_tile(2 * q + j)
                    pool.tensor_tensor(resid[:, b, tt], resid[:, b, tt], bias_b[:], ALU.add).then_inc(biased, 1)

            def pick(u):
                pool.wait_ge(routed, u + 1)
                pool.wait_ge(vc_done, u + 1)
                v = vc[u % 2][:].rearrange("p (a r) -> p a r", r=RANK)
                pool.tensor_tensor(v, v, route[u % 2][:].unsqueeze(2).broadcast_to([P, EXP, RANK]), ALU.mult)\
                    .then_inc(picked, 1)

            def spread(u):
                pool.wait_ge(v_done, u + 1)
                if u >= 2:
                    pool.wait_ge(full["zt"], u - 1)
                pool.tensor_tensor(z[u % 2][:].rearrange("p (a r) -> p a r", r=RANK),
                                   route[u % 2][:].unsqueeze(2).broadcast_to([P, EXP, RANK]),
                                   vr[u % 2][:].unsqueeze(1).broadcast_to([P, EXP, RANK]), ALU.mult).then_inc(z_done, 1)

            parts = {"ws": w_low, "t": cut, "pow": power, "gate": gate, "ab": experts_lo, "x2t": add_bias, "pick": pick,
                     "spread": spread}
            for step in STEPS:
                if step[0] in parts:
                    parts[step[0]](*step[1:])

        @block.vector
        def _(dve):
            count = {"added": 0, "stat": 0, "mv": 0}

            def low(dst, src, high, s):
                dve.tensor_tensor(dst, src, high.bitcast(F32), ALU.subtract).then_inc(s, 1)

            def split_lo(kind, n, dst, src, high):
                dve.wait_ge(hi[kind], n + 1)
                low(dst, src, high, lo[kind])

            def w_low(n):
                if n < 3:
                    a, b = W_CHUNKS[n]
                    dve.wait_ge(w_hi[n], 1)
                    low(w_l[:, a:b], w_raw[:, a:b], w_h[:, a:b], w_lo[n])

            def split_x(b):
                dve.wait_ge(xT_hi, b + 1)
                low(xT_l[b % 2][:], act_raw[:, :, b * S:(b + 1) * S], xT_h[b % 2][:], xT_lo)

            def qk(b):
                split_lo("qk", b, qk_l[:], wide("qk", b)[:].rearrange("p (m s) -> p m s", m=4), qk_h[:])

            def row_max(b, g):
                dve.wait_ge(full["s"], SG * b + g + 1)
                if g < 2:
                    dst, keys = nm[:, 0, 8 * g:8 * g + 8], P
                else:
                    dst, keys = nm[:, 1, 4 * (g - 2):4 * (g - 2) + 4], S
                if b >= 1 and g == 0:
                    dve.wait_ge(nm_lo, b)
                dve.tensor_reduce(dst, wide("s", b, g)[:].rearrange("p (h k) -> p h k", k=keys), AX.X, ALU.max,
                                  negate=True).then_inc(maxed, 1)

            def split_max(b):
                dve.wait_ge(maxed, SG * (b + 1))
                if b >= 1:
                    dve.wait_ge(full["mt"], b)
                dve.tensor_copy(nm_hl[:, :, 0, :], nm[:]).then_inc(nm_hi, 1)
                dve.wait_ge(nm_hi, b + 1)
                low(nm_hl[:, :, 1, :], nm[:], nm_hl[:, :, 0, :], nm_lo)

            def o(b):
                if b >= 1:
                    dve.wait_ge(full["at"], b)
                for t in range(QT):
                    dve.wait_ge(full["o"], 2 * b + t + 1)
                    v = narrow("o", b, t)[:].rearrange("p (h e) -> p h e", e=VW)
                    dve.reciprocal(rden[:, t, :], v[:, :, HD]).then_inc(rden_done, 1)
                    dve.wait_ge(rden_done, 2 * b + t + 1)
                    dve.tensor_tensor(attn[:, t].rearrange("p (h d) -> p h d", d=HD), v[:, :, 0:HD],
                                      rden[:, t, :].unsqueeze(2).broadcast_to([P, NH, HD]), ALU.mult)\
                       .then_inc(attn_done, 1)

            def statistics(key, tiles, eps):
                n, i = len(tiles), NORM_NO[key] % SETS
                if NORM_NO[key] >= SETS:
                    dve.wait_ge(*over(NORMS[NORM_NO[key] - SETS]))
                for j, v in enumerate(tiles):
                    dve.bn_stats(stats[i][:, j], v).then_inc(stat_done, 1)
                count["stat"] += n
                dve.wait_ge(stat_done, count["stat"])
                for j in range(n):
                    dve.bn_aggr(mv[i][:, j], stats[i][:, j]).then_inc(mv_done, 1)
                count["mv"] += n
                dve.wait_ge(mv_done, count["mv"])
                dve.tensor_scalar(var_eps[i][:, 0:n], mv[i][:, 0:n, 1], eps, None, ALU.add).then_inc(var_done, 1)
                if key in ACT_NORMS:
                    dve.tensor_scalar(neg_mean[i][:, 0:n], mv[i][:, 0:n, 0], -1.0, None, ALU.mult).then_inc(neg_done, 1)

            def norm(kind, n):
                if (kind, n) in ACT_NORMS:
                    return
                i = NORM_NO[kind, n] % SETS
                dve.wait_ge(rstd_done, NORM_NO[kind, n] + 1)
                if kind == "n3" and n >= 2:
                    dve.wait_ge(stored[n % 2], 16 * (n // 2))
                for j, (src, dst) in enumerate(norm_ends(kind, n)):
                    dve.tensor_scalar(dst, src, mv[i][:, j, 0:1], rstd[i][:, j:j + 1], ALU.subtract, ALU.mult)\
                       .then_inc(norm_sem[kind, "dve"], 1)

            def add_stats(key, psum, old):
                i, n = SUM_NO[key] % 2, norm_tiles(key)
                if SUM_NO[key] >= 2:
                    dve.wait_ge(*over(SUMS[SUM_NO[key] - 2]))
                dve.tensor_tensor(pre[i][:, 0:n], psum, old, ALU.add).then_inc(added, 1)
                count["added"] += 1
                dve.wait_ge(added, count["added"])
                statistics(key, [pre[i][:, j] for j in range(n)], 1e-5)

            def at(b):
                split_lo("at", b, flat(aT_l[:]), narrow("at", b)[:], flat(aT_h[:]))

            def n1(b):
                dve.wait_ge(full["wo"], b + 1)
                if b == 0:
                    dve.wait_ge(ld_res, 16)
                add_stats(("n1", b), narrow("wo", b)[:].rearrange("p (t d) -> p t d", t=QT), resid[:, b])

            def xt(b):
                split_lo("xt", b, flat(x1T_l[:]), narrow("xt", b)[:], flat(x1T_h[:]))

            def xq(b):
                split_lo("xq", b, xq_l[:, :, b, :], narrow("xq", b)[:].rearrange("p (h s) -> p h s", h=XH),
                         xq_h[:, :, b, :])

            def split_context(c):
                v = slice(c * 512, c * 512 + 512)
                dve.wait_ge(cT_hi, c + 1)
                low(cT_l[:, :, v], act_raw[:, :, v], cT_h[:, :, v], cT_lo)

            def xk(c):
                v = slice(c * 512, c * 512 + 512)
                split_lo("xk", c, xk_l[:, :, v], wide("xk", c)[:].rearrange("p (h s) -> p h s", h=XH), xk_h[:, :, v])

            def xv(c):
                for n in range(2):
                    b = 2 * c + n
                    split_lo("xv", b, xv_l[:, :, :, b, :],
                             wide("xv", c)[:, n * 512:n * 512 + 512].rearrange("p (t h e) -> p t h e", t=QT, h=XH),
                             xv_h[:, :, :, b, :])

            def retention_weights(h):
                if h == 0:
                    dve.wait_ge(ld_dec, 16)
                dve.wait_ge(abs_done, h + 1)
                dve.tensor_tensor(mag[:, h], mag[:, h], dec[:, h], ALU.mult).then_inc(decayed, 1)
                dve.wait_ge(decayed, h + 1)
                dve.tensor_scalar(rA_h[:, h], mag[:, h], 1.0, None, ALU.max).then_inc(rA_hi, 1)
                dve.wait_ge(rA_hi, h + 1)
                dve.scalar_tensor_tensor(out=rA_l[:, h], in0=mag[:, h], scalar=1.0, in1=rA_h[:, h].bitcast(F32),
                                         op0=ALU.max, op1=ALU.subtract).then_inc(rA_lo, 1)

            def gs(t):
                dve.wait_ge(full["ox"], t + 1)
                v = wide("ox", t)[:].rearrange("p (h b e) -> p b h e", h=XH, b=B)
                statistics(("gs", t), [v[:, b] for b in range(B)], 1e-3)

            def gm(t):
                i = NORM_NO["gs", t] % SETS
                dve.wait_ge(gb_done, B)
                v = wide("ox", t)[:].rearrange("p (h b e) -> p b h e", h=XH, b=B)
                for b in range(B):
                    g = gg[:, b, t].rearrange("p (h e) -> p h e", h=XH)
                    dve.scalar_tensor_tensor(out=g, in0=v[:, b], scalar=mv[i][:, b, 0:1], in1=g, op0=ALU.subtract,
                                             op1=ALU.mult).then_inc(y_mul, 1)

            def ga(t):
                i = NORM_NO["gs", t] % SETS
                dve.wait_ge(rstd_done, NORM_NO["gs", t] + 1)
                for b in range(B):
                    dve.wait_ge(y_mul, B * t + b + 1)
                    dve.scalar_tensor_tensor(out=gg[:, b, t], in0=gg[:, b, t], scalar=rstd[i][:, b:b + 1],
                                             in1=gb[:, b, t], op0=ALU.mult, op1=ALU.add).then_inc(y_done, 1)

            def yt(q):
                split_lo("yt", q, flat(yT_l[q % 2][:]), narrow("yt", q)[:], flat(yT_h[q % 2][:]))

            def n2_(q):
                t, b0 = q // 2, 2 * (q % 2)
                dve.wait_ge(full["w2"], q + 1)
                add_stats(("n2", q), narrow("w2", q)[:].rearrange("p (t d) -> p t d", t=2), resid[:, b0:b0 + 2, t])

            def x2t(q):
                split_lo("x2t", q, flat(x2T_l[:, q]), narrow("x2t", q)[:], flat(x2T_h[:, q]))

            def route_tile(u):
                dve.wait_ge(squared, u + 1)
                if u == 0:
                    dve.wait_ge(iota_ready, 1)
                dve.tensor_reduce(n2[:], sq[:].rearrange("p (a r) -> p a r", r=RANK), AX.X, ALU.add).then_inc(n2_done, 1)
                dve.wait_ge(n2_done, u + 1)
                dve.max(top[:], n2[:]).then_inc(top_done, 1)
                dve.wait_ge(top_done, u + 1)
                dve.max_index(idx[:], top[:], n2[:]).then_inc(idx_done, 1)
                dve.wait_ge(idx_done, u + 1)
                dve.tensor_tensor(eq[:], iota[:].unsqueeze(2).broadcast_to([P, EXP, TOPK]),
                                  idx[:, 0:TOPK].unsqueeze(1).broadcast_to([P, EXP, TOPK]), ALU.is_equal)\
                   .then_inc(eq_done, 1)
                dve.wait_ge(eq_done, u + 1)
                if u >= 2:
                    dve.wait_ge(z_done, u - 1)
                dve.tensor_reduce(route[u % 2][:], eq[:], AX.X, ALU.add).then_inc(routed, 1)

            def sum_picked(u):
                dve.wait_ge(picked, u + 1)
                if u >= 2:
                    dve.wait_ge(z_done, u - 1)
                dve.tensor_reduce(vr[u % 2][:], vc[u % 2][:].rearrange("p (a r) -> p r a", r=RANK), AX.X, ALU.add)\
                   .then_inc(v_done, 1)

            def zt(u):
                split_lo("zt", u, flat(zT_l[u % 2][:]), wide("zt", u)[:], flat(zT_h[u % 2][:]))

            def n3(u):
                b, t = ffn_tile(u)
                dve.wait_ge(full["d"], u + 1)
                dve.wait_ge(biased, u + 1)
                add_stats(("n3", u), narrow("db", u)[:, 0:D].unsqueeze(1), resid[:, b, t:t + 1])

            parts = {"xs": split_x, "ws": w_low, "qk": qk, "s": row_max, "nm": split_max, "o": o, "at": at, "n1": n1, "xt": xt,
                     "xq": xq, "cs": split_context, "xk": xk, "xv": xv, "ra": retention_weights, "gs": gs, "gm": gm, "ga": ga, "norm": norm,
                     "yt": yt, "n2": n2_, "x2t": x2t, "route": route_tile, "sum": sum_picked, "zt": zt, "n3": n3}
            for step in STEPS:
                if step[0] in parts:
                    parts[step[0]](*step[1:])

        @block.tensor
        def _(pe):
            def take(*key):
                if key in BEFORE:
                    pe.wait_ge(*released(BEFORE[key]))

            def three(dst, wh, wl, xh, xl, start, stop):
                pe.matmul(dst, wh, xh, start=start, stop=False)
                pe.matmul(dst, wh, xl, start=False, stop=False)
                return pe.matmul(dst, wl, xh, start=False, stop=stop)

            def qk(b):
                take("qk", b)
                if b == 0:
                    pe.wait_ge(pool_const, 6)
                    for _ in range(WARM):
                        pe.matmul(wide("qk", 0)[:, 0:512], ident_bf[:], causal[:].unsqueeze(1).broadcast_to([P, 4, P]),
                                  start=True, stop=True)
                pe.wait_ge(xT_lo, b + 1)
                for m in range(4):
                    if b == 0 and m % 2 == 0:
                        pe.wait_ge(w_lo[m // 2], 1)
                    for k in range(KD):
                        c = W_QK + (m * KD + k) * P
                        mm = three(wide("qk", b)[:, m * S:(m + 1) * S], w_h[:, c:c + P], w_l[:, c:c + P],
                                   xT_h[b % 2][:, k], xT_l[b % 2][:, k], k == 0, k == KD - 1)
                mm.then_inc(full["qk"], 1)

            def by_weights(kind, n, xh, xl, col):
                take(kind, n)
                for t in range(2):
                    for k in range(KD):
                        c = col + k * D
                        mm = three(narrow(kind, n)[:, t * D:(t + 1) * D], xh[:, k, t * P:(t + 1) * P],
                                   xl[:, k, t * P:(t + 1) * P], w_h[:, c:c + D], w_l[:, c:c + D], k == 0, k == KD - 1)
                mm.then_inc(full[kind], 1)

            def v(b):
                if b == 0:
                    pe.wait_ge(w_lo[2], 1)
                by_weights("v", b, xT_h[b % 2], xT_l[b % 2], W_V)

            def s(b, g):
                take("s", b, g)
                if g == 0:
                    pe.wait_ge(stacked[b % 2], 96 * (b // 2 + 1))
                rows = slice(64 * (b % 2), 64 * (b % 2) + HI)
                t, heads, keys = (0, range(8 * g, 8 * g + 8), P) if g < 2 else (1, range(4 * g - 8, 4 * g - 4), S)
                n_bank = 512 // keys
                for n, h in enumerate(heads):
                    pe.matmul(wide("s", b, g)[:, n * keys:(n + 1) * keys], q_st[rows, h, t * P:(t + 1) * P],
                              k_st[rows, h, 0:keys], start=n % n_bank == 0, stop=False)
                    if n % n_bank == n_bank - 1:
                        bank = wide("s", b, g)[:, (n + 1 - n_bank) * keys:(n + 1) * keys]
                        mm = pe.matmul(bank.rearrange("p (h k) -> p h k", h=n_bank)[:, :, keys - P:], ident_bf[:],
                                       causal[:].unsqueeze(1).broadcast_to([P, n_bank, P]), start=False, stop=True)
                mm.then_inc(full["s"], 1)

            def mt(b):
                take("mt", b)
                pe.wait_ge(nm_lo, b + 1)
                for t in range(QT):
                    mm = pe.transpose(narrow("mt", b)[0:2 * NH, t * P:(t + 1) * P],
                                      nm_hl[:, t].rearrange("p a h -> p (a h)").bitcast(F32), ident[:])
                mm.then_inc(full["mt"], 1)

            def t(b, g):
                take("t", b, g)
                if g == 0:
                    pe.wait_ge(nm_stacked[b % 2], 16 * (b // 2 + 1))
                rows = slice(64 * (b % 2), 64 * (b % 2) + HM)
                kt, heads, q0 = (0, range(4 * g, 4 * g + 4), 0) if g < 4 else (1, range(8 * g - 32, 8 * g - 24), P)
                for n, h in enumerate(heads):
                    mm = pe.matmul(wide("t", b, g)[:, n * (S - q0):(n + 1) * (S - q0)], k_st[rows, h, kt * P:(kt + 1) * P],
                                   q_st[rows, h, q0:S], start=True, stop=True)
                mm.then_inc(full["t"], 1)

            def ot(b):
                take("ot", b)
                pe.wait_ge(v_copied, b + 1)
                pe.wait_ge(cut_done, SG * (b + 1))
                vv = vs[b % 2]
                for g in range(4):
                    for kt in range(QT):
                        for j in range(4):
                            h = 4 * g + j
                            dst = wide("ot", b)[32 * j:32 * j + 32, g * S + kt * P:(g + 1) * S]
                            if kt == 0:
                                p = probs[:, g, j * S:(j + 1) * S]
                            else:
                                p = probs[:, 4 + h // 8, (h % 8) * P:(h % 8 + 1) * P]
                            mm = pe.matmul(dst, vv[:, kt, h], p, start=(kt == 0), stop=(kt == QT - 1))
                mm.then_inc(full["ot"], 1)

            def o(b):
                pe.wait_ge(oT_copied, b + 1)
                for t in range(QT):
                    take("o", b, t)
                    for g in range(4):
                        mm = pe.transpose(narrow("o", b, t)[:, g * P:(g + 1) * P], oT[:, g, t * P:(t + 1) * P], ident[:])
                    mm.then_inc(full["o"], 1)

            def turn(kind, n, tiles):
                take(kind, n)
                for k in range(KD):
                    for t in range(2):
                        mm = pe.transpose(narrow(kind, n)[:, k * S + t * P:k * S + (t + 1) * P],
                                          tiles[t][:, k * P:(k + 1) * P], ident[:])
                mm.then_inc(full[kind], 1)

            def at(b):
                pe.wait_ge(attn_done, 2 * b + 2)
                turn("at", b, [attn[:, t] for t in range(QT)])

            def wo(b):
                pe.wait_ge(lo["at"], b + 1)
                if b == 0:
                    pe.wait_ge(w_lo[3], 1)
                by_weights("wo", b, aT_h, aT_l, W_O)

            def xt(b):
                pe.wait_ge(*over(("n1", b)))
                turn("xt", b, [resid[:, b, t] for t in range(QT)])

            def gate(b):
                by_weights("gate", b, x1T_h, x1T_l, W_G)

            def xq(b):
                take("xq", b)
                pe.wait_ge(lo["xt"], b + 1)
                for h in range(XH):
                    c = W_H + h * P
                    mm = three(narrow("xq", b)[:, h * S:(h + 1) * S], w_h[:, c:c + P], w_l[:, c:c + P],
                               x1T_h[:, h], x1T_l[:, h], True, True)
                mm.then_inc(full["xq"], 1)

            def xk(c):
                take("xk", c)
                pe.wait_ge(cT_lo, c + 1)
                for h in range(XH):
                    w0 = W_H + h * P
                    mm = three(wide("xk", c)[:, h * 512:(h + 1) * 512], w_h[:, w0:w0 + P], w_l[:, w0:w0 + P],
                               cT_h[:, h, c * 512:(c + 1) * 512], cT_l[:, h, c * 512:(c + 1) * 512], True, True)
                mm.then_inc(full["xk"], 1)

            def xv(c):
                take("xv", c)
                pe.wait_ge(keys_copied, c + 1)
                for n in range(4):
                    s0 = c * 512 + n * P
                    for h in range(XH):
                        mm = pe.transpose(wide("xv", c)[:, n * 256 + h * P:n * 256 + (h + 1) * P], act_raw[:, h, s0:s0 + P],
                                          ident[:])
                mm.then_inc(full["xv"], 1)

            def sx(h):
                take("sx", h)
                if h == 0:
                    pe.wait_ge(lo["xk"], 2)
                    pe.wait_ge(lo["xq"], B)
                for t in range(QT):
                    q0, c0 = t * P, t * S
                    for b in range(B):
                        k0 = b * S + t * P
                        mm = three(narrow("sx", h)[:, c0:c0 + S - q0], xk_h[:, h, k0:k0 + P], xk_l[:, h, k0:k0 + P],
                                   xq_h[:, h, b, q0:S], xq_l[:, h, b, q0:S], b == 0, b == B - 1)
                mm.then_inc(full["sx"], 1)

            def ox(t):
                take("ox", t)
                pe.wait_ge(lo["xv"], B)
                pe.wait_ge(ones_r_ready, 1)
                for h in range(XH):
                    pe.wait_ge(rA_lo, h + 1)
                    dst = wide("ox", t)[:, h * 512:(h + 1) * 512]
                    v0h, v0l, v1h, v1l = (v_[:, k, h].rearrange("p b e -> p (b e)") for k in range(QT) for v_ in (xv_h, xv_l))
                    three(dst, rA_h[:, h, t * P:(t + 1) * P], rA_l[:, h, t * P:(t + 1) * P], v0h, v0l, True, False)
                    if t == 0:
                        pe.matmul(dst, ones_r[:], v1h, start=False, stop=False)
                        mm = pe.matmul(dst, ones_r[:], v1l, start=False, stop=True)
                    else:
                        mm = three(dst, rA_h[:, h, 256:384], rA_l[:, h, 256:384], v1h, v1l, False, True)
                mm.then_inc(full["ox"], 1)

            def yt(q):
                t_, b0 = q // 2, 2 * (q % 2)
                pe.wait_ge(y_done, B * t_ + b0 + 2)
                turn("yt", q, [gg[:, b0 + j, t_] for j in range(2)])

            def w2(q):
                pe.wait_ge(lo["yt"], q + 1)
                by_weights("w2", q, yT_h[q % 2], yT_l[q % 2], W_O2)

            def x2t(q):
                t_, b0 = q // 2, 2 * (q % 2)
                pe.wait_ge(*over(("n2", q)))
                turn("x2t", q, [resid[:, b0 + j, t_] for j in range(2)])

            def ve(u):
                q, j = u // 2, u % 2
                take("ve", u)
                pe.wait_ge(lo["x2t"], q + 1)
                if u == 0:
                    pe.wait_ge(ab_lo, 2)
                for c in range(2):
                    for k in range(KD):
                        mm = three(wide("ve", u)[:, c * 512:(c + 1) * 512], x2T_h[:, q, k, j * P:(j + 1) * P],
                                   x2T_l[:, q, k, j * P:(j + 1) * P], ea_h[:, k, c * 512:(c + 1) * 512],
                                   ea_l[:, k, c * 512:(c + 1) * 512], k == 0, k == KD - 1)
                mm.then_inc(full["ve"], 1)

            def zt(u):
                take("zt", u)
                pe.wait_ge(z_done, u + 1)
                for k in range(ER // P):
                    mm = pe.transpose(wide("zt", u)[:, k * P:(k + 1) * P], z[u % 2][:, k * P:(k + 1) * P], ident[:])
                mm.then_inc(full["zt"], 1)

            def db(u):
                q, j = u // 2, u % 2
                take("db", u)
                dst = narrow("db", u)[:, 0:D]
                for k in range(KD):
                    c = W_F + k * D
                    three(dst, x2T_h[:, q, k, j * P:(j + 1) * P], x2T_l[:, q, k, j * P:(j + 1) * P],
                          w_h[:, c:c + D], w_l[:, c:c + D], k == 0, False)

            def d(u):
                dst = narrow("db", u)[:, 0:D]
                pe.wait_ge(lo["zt"], u + 1)
                if u == 0:
                    pe.wait_ge(ab_lo, 4)
                for k in range(ER // P):
                    mm = three(dst, zT_h[u % 2][:, k], zT_l[u % 2][:, k], eb_h[:, k], eb_l[:, k], False, k == ER // P - 1)
                mm.then_inc(full["d"], 1)

            parts = {"qk": qk, "v": v, "s": s, "mt": mt, "t": t, "ot": ot, "o": o, "at": at, "wo": wo, "xt": xt,
                     "gate": gate, "xq": xq, "xk": xk, "xv": xv, "sx": sx, "ox": ox, "yt": yt, "w2": w2, "x2t": x2t,
                     "ve": ve, "zt": zt, "db": db, "d": d}
            for step in STEPS:
                if step[0] in parts:
                    parts[step[0]](*step[1:])


def _decay():
    import numpy as np
    idx = np.arange(S, dtype=np.float32)
    out = np.zeros((P, XH, 384), np.float32)
    for h in range(XH):
        gam = np.float64(1.0 - 2.0 ** (-5.0 - h))
        expo = idx[None, :] - idx[:, None]
        d = np.where(expo <= 0, gam ** np.minimum(expo, 0), 0.0)
        d = (d / np.sqrt(d.sum(-1))[None, :] / np.sqrt(128.0)).T.astype(np.float32)
        out[:, h, 0:S] = d[0:P]
        out[:, h, S:] = d[P:, P:]
    return out


def kernel(x, ctx_2048, L0_attn_w_qkv, L0_attn_w_o, L0_xattn_Wh, L0_xattn_wg_w, L0_xattn_wo_w, L0_xattn_gn_gamma,
           L0_xattn_gn_beta, L0_ffn_A, L0_ffn_B, L0_ffn_W, L0_ffn_bias):
    import numpy as np
    import concourse.bacc as bacc
    from concourse.bass_utils import run_bass_kernel_spmd

    def rows(a):
        a = np.asarray(a)
        return a.reshape(a.shape[0] // P, P, a.shape[1]).transpose(1, 0, 2)

    def flat(a):
        return a.reshape(P, -1)

    def heads(a):
        return np.asarray(a).reshape(HB, 2, HD, D).transpose(1, 2, 0, 3).reshape(D, D)

    wqkv = np.asarray(L0_attn_w_qkv)
    wqk = np.concatenate([heads(wqkv[0:D]), heads(wqkv[D:2 * D])], 0)
    wqk = rows(wqk.T).reshape(P, KD, 4, P).transpose(0, 2, 1, 3)
    w = np.concatenate([flat(wqk), flat(rows(wqkv[2 * D:].T)), flat(rows(np.asarray(L0_attn_w_o).T)),
                        flat(np.asarray(L0_xattn_Wh).transpose(1, 0, 2)), flat(rows(L0_xattn_wg_w)),
                        flat(rows(L0_xattn_wo_w)), flat(rows(np.asarray(L0_ffn_W).T))], 1)
    a = np.asarray(L0_ffn_A).reshape(ER, D).T
    b = np.asarray(L0_ffn_B).transpose(0, 2, 1).reshape(ER, D)
    xf, cf = np.asarray(x).reshape(B * S, D), np.asarray(ctx_2048).reshape(B * S, D)
    arrays = {
        "x": np.asarray(x).reshape(B, QT, P, D).transpose(2, 0, 1, 3),
        "xT": rows(xf.T), "cT": rows(cf.T), "w": w, "aT": flat(rows(a)), "bT": flat(rows(b)),
        "gam": np.broadcast_to(np.asarray(L0_xattn_gn_gamma), (P, D)),
        "bet": np.broadcast_to(np.asarray(L0_xattn_gn_beta), (P, D)),
        "bias": np.broadcast_to(np.asarray(L0_ffn_bias), (P, D)),
        "decay": _decay(),
    }
    arrays = {k + "_dram": np.ascontiguousarray(v) for k, v in arrays.items()}
    nc = bacc.Bacc("TRN2", target_bir_lowering=False, num_devices=1)
    args = [nc.dram_tensor(k, v.shape, mybir.dt.from_np(v.dtype), kind="ExternalInput").ap() for k, v in arrays.items()]
    args.append(nc.dram_tensor("out_dram", (P, B, QT, D), F32, kind="ExternalOutput").ap())
    decoder_layer(nc, *args)
    r = run_bass_kernel_spmd(nc, [arrays], core_ids=[0])
    got = r.results[0]["out_dram"]
    return np.ascontiguousarray(got.transpose(1, 2, 0, 3).reshape(B, S, D))
```
